# Optimizing a Trainium2 kernel written in Bass

```python
import numpy as np
import jax
import jax.numpy as jnp

def _softmax(x, axis=-1):
    return jax.nn.softmax(x, axis=axis)

def _gelu(x):
    return jax.nn.gelu(x, approximate=True)

def _silu(x):
    return jax.nn.silu(x)

def _sigmoid(x):
    return jax.nn.sigmoid(x)

def _layernorm(x, axis=-1, eps=1e-05):
    m = jnp.mean(x, axis=axis, keepdims=True)
    v = jnp.var(x, axis=axis, keepdims=True)
    return (x - m) / jnp.sqrt(v + eps)

def _scatter_add(tgt, idx, src, axis=0):
    return tgt.at[idx].add(src)

def _segment_sum(src, seg, n):
    return jax.ops.segment_sum(src, seg, n)
kernel_name = 'mk_seq_postln_d1_jaxref_r8_7f47a7'

def setup_inputs(seed: int=0):
    np.random.seed(seed)
    _w = jnp.asarray

    def _L0_attn_setup():
        import jax, jax.numpy as jnp
        import numpy as np
        import math
        D_MODEL, HEADS, KQ = (128, 16, 64)
        B, S = (4, 256)
        key = jax.random.key(seed)
        k0, k1, k2, k3, k4 = jax.random.split(key, 5)
        scale = D_MODEL ** (-0.5)
        return {'x_BSE': jax.random.normal(k0, (B, S, D_MODEL), dtype=jnp.float32), 'w_q': jax.random.normal(k1, (D_MODEL, HEADS, KQ), dtype=jnp.float32) * scale, 'w_k': jax.random.normal(k2, (D_MODEL, HEADS, KQ), dtype=jnp.float32) * scale, 'w_v': jax.random.normal(k3, (D_MODEL, HEADS, KQ), dtype=jnp.float32) * scale, 'w_o': jax.random.normal(k4, (D_MODEL, HEADS, KQ), dtype=jnp.float32) * scale}
    _L0_attn_in = _L0_attn_setup()

    def _L0_ffn_setup():
        import jax, jax.numpy as jnp
        import numpy as np
        D_MODEL = 128
        EXPANSION = 4
        D_HIDDEN = D_MODEL * EXPANSION
        NUM_STAGES = int(np.log2(D_HIDDEN))

        def butterfly(y, weights, dim):
            lead = y.shape[:-1]
            for stage in range(weights.shape[0]):
                s = 2 ** stage
                nb = dim // (2 * s)
                yr = y.reshape(*lead, nb, 2, s)
                a = yr[..., 0, :]
                b = yr[..., 1, :]
                w = weights[stage].reshape(nb, s, 2, 2)
                na = w[..., 0, 0] * a + w[..., 0, 1] * b
                nb2 = w[..., 1, 0] * a + w[..., 1, 1] * b
                y = jnp.stack([na, nb2], axis=-2).reshape(*lead, dim)
            return y
        key = jax.random.key(seed)
        ks = jax.random.split(key, 6)
        B, S = (4, 256)
        x = jax.random.normal(ks[0], (B, S, D_MODEL), jnp.float32)
        W_exp = jax.random.normal(ks[1], (D_MODEL, D_HIDDEN), jnp.float32) * 0.02
        b_exp = jnp.zeros((D_HIDDEN,), jnp.float32)
        up_weights = jax.random.normal(ks[2], (NUM_STAGES, D_HIDDEN // 2, 2, 2), jnp.float32) * 0.02
        up_bias = jnp.zeros((D_HIDDEN,), jnp.float32)
        down_weights = jax.random.normal(ks[3], (NUM_STAGES, D_HIDDEN // 2, 2, 2), jnp.float32) * 0.02
        W_con = jax.random.normal(ks[4], (D_HIDDEN, D_MODEL), jnp.float32) * 0.02
        b_con = jnp.zeros((D_MODEL,), jnp.float32)
        down_bias = jnp.zeros((D_MODEL,), jnp.float32)
        return dict(x=x, W_exp=W_exp, b_exp=b_exp, up_weights=up_weights, up_bias=up_bias, down_weights=down_weights, W_con=W_con, b_con=b_con, down_bias=down_bias)
    _L0_ffn_in = _L0_ffn_setup()
    _d = {'L0_attn_x_BSE': _L0_attn_in['x_BSE'], 'L0_attn_w_q': _L0_attn_in['w_q'], 'L0_attn_w_k': _L0_attn_in['w_k'], 'L0_attn_w_v': _L0_attn_in['w_v'], 'L0_attn_w_o': _L0_attn_in['w_o'], 'L0_ffn_W_exp': _L0_ffn_in['W_exp'], 'L0_ffn_b_exp': _L0_ffn_in['b_exp'], 'L0_ffn_up_weights': _L0_ffn_in['up_weights'], 'L0_ffn_up_bias': _L0_ffn_in['up_bias'], 'L0_ffn_down_weights': _L0_ffn_in['down_weights'], 'L0_ffn_W_con': _L0_ffn_in['W_con'], 'L0_ffn_b_con': _L0_ffn_in['b_con'], 'L0_ffn_down_bias': _L0_ffn_in['down_bias']}
    _x0 = _d['L0_attn_x_BSE']
    _d['L0_attn_x_BSE'] = jax.random.normal(jax.random.fold_in(jax.random.key(seed), 1), (4, 1024, 128), dtype=_x0.dtype)
    del _x0
    return _d

def reference(L0_attn_x_BSE, L0_attn_w_q, L0_attn_w_k, L0_attn_w_v, L0_attn_w_o, L0_ffn_W_exp, L0_ffn_b_exp, L0_ffn_up_weights, L0_ffn_up_bias, L0_ffn_down_weights, L0_ffn_W_con, L0_ffn_b_con, L0_ffn_down_bias):

    def _L0_attn_ref(x_BSE, w_q, w_k, w_v, w_o):
        import jax, jax.numpy as jnp
        import numpy as np
        import math
        D_MODEL, HEADS, KQ = (128, 16, 64)
        B, S = (4, 256)
        q_BSHK = jnp.einsum('BSE,EHK->BSHK', x_BSE, w_q)
        k_BMHK = jnp.einsum('BSE,EHK->BSHK', x_BSE, w_k)
        v_BMHK = jnp.einsum('BSE,EHK->BSHK', x_BSE, w_v)
        Kq = q_BSHK.shape[-1]
        logits_BSHM = jnp.einsum('BSHK,BMHK->BSHM', q_BSHK, k_BMHK) / math.sqrt(Kq)
        Sdim = logits_BSHM.shape[1]
        qpos = jnp.arange(Sdim)[:, None]
        mpos = jnp.arange(Sdim)[None, :]
        mask = jnp.where(qpos >= mpos, 0.0, -jnp.inf)[None, :, None, :]
        probs_BSHM = jax.nn.softmax(logits_BSHM + mask, axis=3)
        out_BSHK = jnp.einsum('BSHM,BMHK->BSHK', probs_BSHM, v_BMHK)
        return jnp.einsum('BSHK,EHK->BSE', out_BSHK, w_o)

    def _L0_ffn_ref(x, W_exp, b_exp, up_weights, up_bias, down_weights, W_con, b_con, down_bias):
        import jax, jax.numpy as jnp
        import numpy as np
        D_MODEL = 128
        EXPANSION = 4
        D_HIDDEN = D_MODEL * EXPANSION
        NUM_STAGES = int(np.log2(D_HIDDEN))

        def butterfly(y, weights, dim):
            lead = y.shape[:-1]
            for stage in range(weights.shape[0]):
                s = 2 ** stage
                nb = dim // (2 * s)
                yr = y.reshape(*lead, nb, 2, s)
                a = yr[..., 0, :]
                b = yr[..., 1, :]
                w = weights[stage].reshape(nb, s, 2, 2)
                na = w[..., 0, 0] * a + w[..., 0, 1] * b
                nb2 = w[..., 1, 0] * a + w[..., 1, 1] * b
                y = jnp.stack([na, nb2], axis=-2).reshape(*lead, dim)
            return y
        h = jnp.einsum('bsd,dh->bsh', x, W_exp) + b_exp
        h = butterfly(h, up_weights, D_HIDDEN)
        h = jax.nn.gelu(h + up_bias, approximate=False)
        h = butterfly(h, down_weights, D_HIDDEN)
        y = jnp.einsum('bsh,hd->bsd', h, W_con) + b_con
        return y + down_bias
    x = L0_attn_x_BSE
    x = _layernorm(x + _L0_attn_ref(x, L0_attn_w_q, L0_attn_w_k, L0_attn_w_v, L0_attn_w_o), axis=-1)
    x = _layernorm(x + _L0_ffn_ref(x, L0_ffn_W_exp, L0_ffn_b_exp, L0_ffn_up_weights, L0_ffn_up_bias, L0_ffn_down_weights, L0_ffn_W_con, L0_ffn_b_con, L0_ffn_down_bias), axis=-1)
    return x

_drawn_inputs = setup_inputs


def setup_inputs(seed=0):
    import zlib

    import numpy as np

    out = dict(_drawn_inputs(seed))
    spreads = {'L0_ffn_b_exp': (0.0, 0.1),
     'L0_ffn_up_bias': (0.0, 0.1),
     'L0_ffn_b_con': (0.0, 0.1),
     'L0_ffn_down_bias': (0.0, 0.1)}
    factors = {}
    for name, (base, spread) in spreads.items():
        noise = np.random.default_rng([zlib.crc32(name.encode()), seed]).standard_normal(out[name].shape)
        drawn = base * np.exp(spread * noise) if base else spread * noise
        out[name] = jnp.asarray(drawn.astype(out[name].dtype))
    for name, factor in factors.items():
        out[name] = (out[name] * factor).astype(out[name].dtype)
    return out
```

```python
from contextlib import ExitStack

import concourse.bass as bass
from concourse import mybir
from concourse.alu_op_type import AluOpType as ALU

ACT = mybir.ActivationFunctionType
F32 = mybir.dt.float32
F32R = mybir.dt.float32r
AX_X = mybir.AxisListType.X

P = 128
B, S, D = 4, 1024, 128
H, K = 16, 64
PAIRS = H // 2
UNITS = B * PAIRS
TILES = S // P
CH = 512
CHUNKS = S // CH
TPC = CH // P
HID = 512
HT = HID // P
STAGES = 9
EPS = 1e-5
LOWEST = -3.0e38

STEPS = [(qc, kt) for qc in range(CHUNKS) for kt in range(TPC * (qc + 1))]
NS = len(STEPS)
START = [max(0, kt * P - qc * CH) for qc, kt in STEPS]
DIAG = [kt >= TPC * qc for qc, kt in STEPS]
ND = sum(DIAG)
ADDS = [kt > 0 for _, kt in STEPS]
NA = sum(ADDS)
LAG = 2
PRING = 3
LAST_OF = [max(s for s in range(NS) if STEPS[s][0] == qc) for qc in range(CHUNKS)]
FIRST_OF = [min(s for s in range(NS) if STEPS[s][0] == qc) for qc in range(CHUNKS)]


def diags_until(s):
    return sum(DIAG[:s])


def adds_until(s):
    return sum(ADDS[:s]) if s >= 0 else -sum(ADDS[s:])


MAXES = [("max", h, qt, part) for h in range(2) for qt in range(TILES) for part in range(qt * P // CH + 1)]
FILL = [[] for _ in range(NS)]
FILL[0] = [("proj", 0, 0), ("proj", 1, 0)]
FILL[1] = [("proj", 0, 1), ("proj", 1, 1)]
FILL[2] = [("norm", 1, 1), ("proj", 2, 0), ("proj", 2, 1)]
FILL[3] = [("vt", 0)] + MAXES[0:2]
FILL[4] = [("vt", 1)] + MAXES[2:6]
FILL[5] = MAXES[6:11]
FILL[6] = [("norm", 0, 0)] + MAXES[11:15]
FILL[7] = MAXES[15:20]
FILL[8] = MAXES[20:24]
FILL[9] = [("mt",)]
assert sum(f[0] == "max" for fs in FILL for f in fs) == len(MAXES)
NF = sum(map(len, FILL))
PREFETCH = [f for fs in FILL for f in fs if f[0] != "norm"]
PER_BATCH = PAIRS * NF + CHUNKS


class At:

    def __init__(self, c, cb=0, cj=0, b=None, j=None):
        self.c, self.cb, self.cj, self.b, self.j = c, cb, cj, b, j

    def __add__(self, n):
        return At(self.c + n, self.cb, self.cj, self.b, self.j)

    def times(self, n):
        return At(self.c * n, self.cb * n, self.cj * n, self.b, self.j)

    def half(self):
        assert self.cb % 2 == 0 and self.cj % 2 == 0
        return At(self.c // 2, self.cb // 2, self.cj // 2, self.b, self.j)

    def value(self):
        v = 0
        if self.b is not None and self.cb:
            v = self.b * self.cb
        if self.j is not None and self.cj:
            v = self.j * self.cj + v
        v = v + self.c
        return v


def butterfly_stage(eng, y, first, second, w, stage, rows):
    s = 2 ** stage
    pairs = y.rearrange("p (n i s) -> p n s i", i=2, s=s)
    w = w.rearrange("p (n s o i) -> p n s o i", s=s, o=2, i=2)
    shape = "p (n s o) -> p n s o"
    f, g = first.rearrange(shape, s=s, o=2), second.rearrange(shape, s=s, o=2)
    n = HID // 2 // s

    def product(dst, i):
        src = pairs[:, :, :, i:i + 1].broadcast_to([y.shape[0], n, s, 2])
        wt = w[:, :, :, :, i] if rows else w[:, :, :, i, :]
        return eng.tensor_tensor(dst, src, wt, ALU.mult)

    return [lambda: product(f, 0), lambda: product(g, 1), lambda: eng.tensor_tensor(pairs, f, g, ALU.add)]


def post_norm_layer(nc, x, w_q, w_k, w_v, w_o, W_exp, b_exp, up_w, up_b, down_w, W_con, b_con, down_b, out):
    ctx = ExitStack()
    with ctx:
        def sb(name, shape, dt=F32):
            return ctx.enter_context(nc.sbuf_tensor(name, shape, dt))

        def sem(name):
            return ctx.enter_context(nc.semaphore(name))

        X = sb("X", [P, B * TILES, D])
        XTH = sb("XTH", [P, B * S], F32R)
        XTL = sb("XTL", [P, B * S], F32R)
        WQKV = sb("WQKV", [P, 3, H * K])
        WOT = sb("WOT", [P, PAIRS, D])
        OT = sb("OT", [P, PAIRS, S])
        QH = sb("QH", [P, 2, 2, S], F32R)
        QL = sb("QL", [P, 2, 2, S], F32R)
        KHL = sb("KHL", [P, 2, 2, S], F32R)
        KH1 = sb("KH1", [P, 2, 2, S], F32R)
        PR = sb("PR", [P, PRING, 2, CH])
        SUM = sb("SUM", [P, CHUNKS, 2, CH])
        VP = sb("VP", [P, 2, TILES, 2 * K])
        VT = sb("VT", [P, CHUNKS, CH])
        WST = sb("WST", [P, 2, 3, P], F32R)
        CMASK = sb("CMASK", [P, CH])
        IDN = sb("IDN", [P, P])
        ONES = sb("ONES", [P, K])
        R = sb("R", [P, CH])
        MP = sb("MP", [P, 2 * TILES, 2])
        NEGM = sb("NEGM", [P, 2 * TILES])
        NROW = sb("NROW", [2 * TILES, P], F32R)
        MV = sb("MV", [P, B * TILES, 2])
        MVT = sb("MVT", [P, TPC, 2])
        BS = sb("BS", [P, TPC, 6])
        RSTD = sb("RSTD", [P, B * TILES])
        W1 = sb("W1", [P, HID])
        W2 = sb("W2", [P, HT, D])
        BC = sb("BC", [P, D])
        BIAS1 = sb("BIAS1", [P, HT])
        BROW = sb("BROW", [1, HID])
        EPST = sb("EPST", [P, 1])

        WST_SLOTS = 8
        stage_w = OT[:, :, :]
        w_raw = PR[:, :, :, :].rearrange("p a h c -> p (a h c)")
        wo_nat = w_raw[:, 0:1024]
        wcon_nat = w_raw[:, 1024:1536].rearrange("p (t d) -> p t d", t=HT)
        w2t = w_raw[:, 1536:2048]
        bias_rows = w_raw[0:1, 2048:3072]
        fly = SUM[:, :, :, :].rearrange("p a h c -> p (a h c)")
        fly_a, fly_b = fly[:, 0:HID], fly[:, HID:2 * HID]
        rfly_a, rfly_b = fly[0:1, 2 * HID:3 * HID], fly[0:1, 3 * HID:4 * HID]
        down_row = VT[:, 0, 0:D]
        ot_flat = OT[:, :, :].rearrange("p a s -> p (a s)")
        x1T = [ot_flat[:, i * CH:(i + 1) * CH] for i in range(2)]
        G = [ot_flat[:, (2 + HT * i) * CH:(2 + HT * i + HT) * CH].rearrange("p (t c) -> p t c", t=HT) for i in range(2)]

        SC = [ctx.enter_context(nc.psum_tensor(f"SC{i}", [P, 2, CH], F32)) for i in range(2)]
        O = [ctx.enter_context(nc.psum_tensor(f"O{i}", [P, CH], F32)) for i in range(2)]
        WORK = [ctx.enter_context(nc.psum_tensor(f"WORK{i}", [P, CH], F32)) for i in range(2)]

        in_x, in_w, in_mlp = [sem("in_x0"), sem("in_x1")], sem("in_w"), sem("in_mlp")
        stage_in = [sem(f"stage_in{i}") for i in range(WST_SLOTS)]
        stage_used, stage_used_row = sem("stage_used"), sem("stage_used_row")
        consts_set = sem("consts_set")
        rows_set = sem("rows_set")
        idn_set = sem("idn_set")
        pool_passed, dve_passed = sem("pool_passed"), sem("dve_passed")
        pool_self, dve_self = sem("pool_self"), sem("dve_self")
        xt_made, xt_hi, xt_lo = sem("xt_made"), sem("xt_hi"), sem("xt_lo")
        wt_made, wt_copied = sem("wt_made"), sem("wt_copied")
        w2t_made, w2_made, w2_copied = sem("w2t_made"), sem("w2_made"), sem("w2_copied")
        brow_made, bias_made, bias_copied = sem("brow_made"), sem("bias_made"), sem("bias_copied")
        wq_scaled = sem("wq_scaled")
        weights_hi, weights_lo = sem("weights_hi"), sem("weights_lo")
        work_ready = sem("work_ready")
        work_free = [sem("work_free0"), sem("work_free1")]
        qk_hi = sem("qk_hi")
        negm_made, nrow_made, m_landed = sem("negm_made"), sem("nrow_made"), sem("m_landed")
        scores_ready, exp_done, mask_done = sem("scores_ready"), sem("exp_done"), sem("mask_done")
        pv_done, add_done, o_free = sem("pv_done"), sem("add_done"), sem("o_free")
        h1_added, stats_made = sem("h1_added"), sem("stats_made")
        aggregated = sem("aggregated")
        var_ready, std_made = sem("var_ready"), sem("std_made")
        x1_made, x1t_made, x1t_copied = sem("x1_made"), sem("x1t_made"), sem("x1t_copied")
        hid_ready, gelu_done, y_ready, h2_made = sem("hid_ready"), sem("gelu_done"), sem("y_ready"), sem("h2_made")
        out_made, out_stored = sem("out_made"), sem("out_stored")

        EXP_CREDIT, PV_CREDIT, ADD_CREDIT, O_CREDIT = 2, PRING, PRING, 2

        x_tiles = x.rearrange("b (t p) d -> p (b t) d", p=P)
        out_tiles = out.rearrange("b (t p) d -> p (b t) d", p=P)

        def unit_at(b, j, par):
            return At(par, PAIRS, 2, b, j)

        def work_base(b, j, par):
            first = j is None and par == 0
            return At(len(PREFETCH) + NF * par - (not first), PER_BATCH, 2 * NF, b, j)

        def fillers(first):
            n, made = 0, []
            for s, fs in enumerate(FILL):
                for f in fs:
                    if first and f == ("norm", 1, 1):
                        continue
                    made.append((s, f, n))
                    n += 1
            return made

        def next_tokens(b, j, par):
            if par == 0:
                return b * S
            if j is None:
                return b * S
            return ((b * PAIRS + j * 2 + (par + 1)) // PAIRS % B) * S

        def pair_col(j, par, ahead):
            if j is None:
                return (par + ahead) % PAIRS * P
            return ((j * 2 + (par + ahead)) % PAIRS) * P

        def keys_of(part, qt):
            lo = part * CH
            return lo, min(CH, (qt + 1) * P - lo)

        def prob(s, n=None):
            qc, kt = STEPS[s]
            n = CH - START[s] if n is None else n
            return SUM[:, qc, :, 0:n] if kt == 0 else PR[:, s % PRING, :, 0:n]

        block = ctx.enter_context(nc.Block())

        @block.sync
        def _(sp):
            sp.dma_start(X[:, 0:TILES, :], x_tiles[:, 0:TILES, :]).then_inc(in_x[0], 16)
            for n, w in enumerate((w_q, w_k, w_v)):
                sp.dma_start(WQKV[:, n, :], w.rearrange("e h k -> e (h k)")).then_inc(in_w, 16)
            sp.dma_start(X[:, TILES:, :], x_tiles[:, TILES:, :]).then_inc(in_x[1], 16)
            sp.dma_start(wo_nat, w_o.rearrange("e h k -> e (h k)")).then_inc(in_w, 16)
            sp.dma_start(W1[:, :], W_exp).then_inc(in_mlp, 16)
            sp.dma_start(wcon_nat, W_con.rearrange("(t p) d -> p t d", p=P)).then_inc(in_mlp, 16)
            sp.dma_start(BROW[:, :], b_exp.rearrange("(a n) -> a n", a=1)).then_inc(in_mlp, 16)
            sp.dma_start(bias_rows[:, 0:HID], up_b.rearrange("(a n) -> a n", a=1)).then_inc(in_mlp, 16)
            sp.dma_start(BC[:, :], b_con.rearrange("(a n) -> a n", a=1).broadcast_to([P, D])).then_inc(in_mlp, 16)
            sp.dma_start(down_row, down_b.rearrange("(a n) -> a n", a=1).broadcast_to([P, D])).then_inc(in_mlp, 16)
            for n in range(2 * STAGES):
                w, st = (up_w, n) if n < STAGES else (down_w, 2 * STAGES - 1 - n)
                if n >= WST_SLOTS:
                    sp.wait_ge(stage_used, n - WST_SLOTS + 1)
                    sp.wait_ge(stage_used_row, min(n - WST_SLOTS + 1, STAGES))
                src = w[st:st + 1].rearrange("a k i o -> a (k i o)").broadcast_to([P, 2 * HID])
                sp.dma_start(stage_w[:, n % WST_SLOTS, :], src).then_inc(stage_in[n % WST_SLOTS], 16)

            def rows(par, f_unit):
                sp.wait_ge(nrow_made, (f_unit + 1).value())
                for h in range(2):
                    row = K if h == 0 else 0
                    dst = QL[row:row + 1, par, h, :].rearrange("a (t c) -> a t c", t=TILES)
                    sp.dma_start(dst.bitcast(F32), NROW[h * TILES:(h + 1) * TILES, :].bitcast(F32)).then_inc(m_landed, 16)

            rows(0, At(0))
            with sp.Fori(0, B) as b:
                for par in range(2):
                    rows(1 - par, unit_at(b, None, par) + 1)
                with sp.Fori(1, PAIRS // 2) as j:
                    for par in range(2):
                        rows(1 - par, unit_at(b, j, par) + 1)
            sp.wait_ge(m_landed, 32 * (UNITS + 1))
            for n in range(B):
                sp.wait_ge(out_made, (n + 1) * TILES)
                sp.dma_start(out_tiles[:, n * TILES:(n + 1) * TILES, :],
                             X[:, n * TILES:(n + 1) * TILES, :]).then_inc(out_stored, 16)
            sp.wait_ge(out_stored, 16 * B)

        @block.gpsimd
        def _(pool):
            nc.gpsimd.memset(IDN[:], 0.0).then_inc(pool_self, 1)
            nc.gpsimd.memset(CMASK[:], 0.0).then_inc(pool_self, 1)
            pool.wait_ge(pool_self, 1)
            nc.gpsimd.affine_select(out=IDN[:], in_=IDN[:], compare_op=ALU.not_equal, fill=1.0, base=0,
                                    pattern=[[-1, P]], channel_multiplier=1).then_inc(idn_set, 1)
            pool.wait_ge(pool_self, 2)
            nc.gpsimd.affine_select(out=CMASK[:, CH - P:], in_=CMASK[:, CH - P:], compare_op=ALU.is_ge, fill=LOWEST,
                                    base=0, pattern=[[-1, P]], channel_multiplier=1).then_inc(consts_set, 1)
            nc.gpsimd.memset(ONES[:], 1.0).then_inc(consts_set, 1)
            nc.gpsimd.memset(EPST[:], EPS).then_inc(consts_set, 1)
            pool.sem_inc(add_done, ADD_CREDIT)
            pool_n = 2
            pool.wait_ge(in_mlp, 16 * 6)
            for st in range(STAGES):
                pool.wait_ge(stage_in[st % WST_SLOTS], 16 * (st // WST_SLOTS + 1))
                ops = butterfly_stage(nc.gpsimd, BROW[:, :], rfly_a, rfly_b, stage_w[0:1, st % WST_SLOTS, :], st, True)
                for n, op in enumerate(ops):
                    op().then_inc(pool_self, 1)
                    pool_n += 1
                    if n > 0:
                        pool.wait_ge(pool_self, pool_n)
                pool.sem_inc(stage_used_row, 1)
            nc.gpsimd.tensor_tensor(BROW[:, :], BROW[:, :], bias_rows[:, 0:HID], ALU.add).then_inc(brow_made, 1)

            fill = nc.gpsimd.to_reg(0.0)

            def mask(unit, s):
                if not DIAG[s]:
                    return
                pool.wait_ge(exp_done, (unit.times(NS) + (s + 1 + EXP_CREDIT)).value())
                pool.sem_inc(pool_passed, 1)
                tri = prob(s, P)
                nc.gpsimd.affine_select(out=tri, in_=tri, compare_op=ALU.is_ge, fill=fill, base=0,
                                        pattern=[[0, 2], [1, P]], channel_multiplier=-1).then_inc(mask_done, 1)

            def add(unit, s):
                if not ADDS[s]:
                    return
                qc = STEPS[s][0]
                if DIAG[s]:
                    pool.wait_ge(mask_done, (unit.times(ND) + diags_until(s + 1)).value())
                else:
                    pool.wait_ge(exp_done, (unit.times(NS) + (s + 1 + EXP_CREDIT)).value())
                pool.wait_ge(pv_done, (unit.times(NS) + (FIRST_OF[qc] + 1 + PV_CREDIT)).value())
                pool.wait_ge(add_done, (unit.times(NA) + (adds_until(s) + ADD_CREDIT)).value())
                total = SUM[:, qc, :, START[s]:]
                nc.gpsimd.tensor_tensor(total, total, prob(s), ALU.add).then_inc(add_done, 1)

            def window(b, j, par, first):
                unit = unit_at(b, j, par)
                for s in range(NS):
                    mask(unit, s)
                    if s > 0:
                        add(unit, s - 1)
                add(unit, NS - 1)

            with pool.Fori(0, B) as b:
                for par in range(2):
                    window(b, None, par, par == 0)
                with pool.Fori(1, PAIRS // 2) as j:
                    for par in range(2):
                        window(b, j, par, False)

        @block.tensor
        def _(pe):
            pe.wait_ge(idn_set, 1)
            banks = [SC[0][:, 0, :], SC[0][:, 1, :], SC[1][:, 0, :], SC[1][:, 1, :]]
            for g in range(B * CHUNKS):
                pe.wait_ge(in_x[g >= CHUNKS], 16)
                if g >= 4:
                    pe.wait_ge(xt_lo, g - 3)
                for i in range(TPC):
                    t = nc.tensor.transpose(banks[g % 4][:, i * P:(i + 1) * P], X[:, g * TPC + i, :], IDN[:])
                t.then_inc(xt_made, 1)
            pe.wait_ge(in_w, 64)
            for g in range(2):
                for i in range(TPC):
                    n = g * TPC + i
                    t = nc.tensor.transpose(O[g][:, i * P:(i + 1) * P], wo_nat[:, n * P:(n + 1) * P], IDN[:])
                t.then_inc(wt_made, 1)
            pe.wait_ge(in_mlp, 16 * 6)
            pe.wait_ge(wt_copied, 1)
            for i in range(HT):
                t = nc.tensor.transpose(O[0][:, i * P:(i + 1) * P], wcon_nat[:, i, :], IDN[:])
            t.then_inc(w2t_made, 1)
            pe.wait_ge(wt_copied, 4)
            for i in range(HT):
                t = nc.tensor.transpose(O[1][:, i * P:(i + 1) * P], w2t[:, i * P:(i + 1) * P], IDN[:])
            t.then_inc(w2_made, 1)
            pe.wait_ge(brow_made, 1)
            for i in range(HT):
                t = nc.tensor.matmul(O[0][:, i:i + 1], BROW[:, i * P:(i + 1) * P], ONES[0:1, 0:1], start=True, stop=True)
            t.then_inc(bias_made, 1)
            pe.wait_ge(w2_copied, 2)

            def take_work(at, c):
                if not (at.b is None and c < 2):
                    pe.wait_ge(work_free[c % 2], at.half().value())
                return WORK[c % 2]

            def qk_mm(dst, h, buf, lhs, rhs, kt, q0, n, start):
                return nc.tensor.matmul(dst, lhs[:, buf, h, kt * P:(kt + 1) * P], rhs[:, buf, h, q0:q0 + n],
                                        start=start, stop=not start)

            def filler(f, at, unit, nxt, tokens):
                w = take_work(at, at.c)
                if f[0] == "proj":
                    _, n, c = f
                    if f == ("proj", 0, 0):
                        pe.wait_ge(weights_lo, (unit + 2).value())
                    cols = bass.ds(tokens + c * CH, CH)
                    nc.tensor.matmul(w[:, :], WST[:, 0, n, :], XTH[:, cols], start=True, stop=False)
                    nc.tensor.matmul(w[:, :], WST[:, 1, n, :], XTH[:, cols], start=False, stop=False)
                    t = nc.tensor.matmul(w[:, :], WST[:, 0, n, :], XTL[:, cols], start=False, stop=True)
                elif f[0] == "vt":
                    c = f[1]
                    for i in range(TPC):
                        t = nc.tensor.transpose(w[:, i * P:(i + 1) * P], VT[:, c, i * P:(i + 1) * P], IDN[:])
                elif f[0] == "max":
                    _, h, qt, part = f
                    lo, n = keys_of(part, qt)
                    t = nc.tensor.matmul(w[:, 0:n], QH[:, nxt, h, qt * P:(qt + 1) * P], KHL[:, nxt, h, lo:lo + n],
                                         start=True, stop=True)
                elif f[0] == "mt":
                    pe.wait_ge(negm_made, (unit + 2).value())
                    t = nc.tensor.transpose(w[0:2 * TILES, 0:P], NEGM[:, :], IDN[:])
                else:
                    norm(f, w, unit)
                    return
                t.then_inc(work_ready, 1)

            def norm(f, w, unit):
                _, qc, before = f
                pe.wait_ge(add_done, ((unit + -before).times(NA) + (adds_until(LAST_OF[qc] + 1) + ADD_CREDIT)).value())
                for h in range(2):
                    t = nc.tensor.matmul(w[h * K:(h + 1) * K, :], ONES[:, :], SUM[:, qc, h, :], start=True, stop=True)
                t.then_inc(work_ready, 1)

            def scores(unit, par, s, between):
                qc, kt = STEPS[s]
                q0, n = qc * CH + START[s], CH - START[s]
                pe.wait_ge(exp_done, (unit.times(NS) + (s + 1)).value())
                for h in range(2):
                    dst = SC[s % 2][:, h, 0:n]
                    nc.tensor.matmul(dst, KHL[:, par, h, kt * P:(kt + 1) * P], QH[:, par, h, q0:q0 + n],
                                     start=True, stop=False)
                    if s == 0 and h == 0:
                        pe.wait_ge(m_landed, ((unit + 1).times(32)).value())
                    t = nc.tensor.matmul(dst, KH1[:, par, h, kt * P:(kt + 1) * P], QL[:, par, h, q0:q0 + n],
                                         start=False, stop=True)
                    if h == 0:
                        between()
                t.then_inc(scores_ready, 1)

            def pv(unit, par, s):
                qc, kt = STEPS[s]
                n = CH - START[s]
                if kt == 0:
                    pe.wait_ge(o_free, (unit.times(CHUNKS) + (qc + 1)).value())
                if DIAG[s]:
                    pe.wait_ge(mask_done, (unit.times(ND) + diags_until(s + 1)).value())
                else:
                    pe.wait_ge(exp_done, (unit.times(NS) + (s + 1 + EXP_CREDIT)).value())
                p = prob(s)
                for h in range(2):
                    t = nc.tensor.matmul(O[qc][h * K:(h + 1) * K, START[s]:], VP[:, par, kt, h * K:(h + 1) * K],
                                         p[:, h, :], start=kt == 0, stop=s == LAST_OF[qc])
                t.then_inc(pv_done, 1)

            def window(b, j, par, first):
                unit, base, tokens = unit_at(b, j, par), work_base(b, j, par), next_tokens(b, j, par)
                queue = fillers(first)
                for s in range(NS):
                    mine = [(f, n) for at, f, n in queue if at == s]

                    def fill(k):
                        for f, n in mine[:k]:
                            filler(f, base + n, unit, 1 - par, tokens)
                        del mine[:k]

                    scores(unit, par, s, lambda: fill(1))
                    fill(1)
                    if s >= LAG:
                        pv(unit, par, s - LAG)
                    elif not first:
                        pv(unit + -1, 1 - par, NS + s - LAG)
                    fill(len(mine))

            def flush(b):
                unit = At(PAIRS - 1, PAIRS, 0, b)
                for s in range(NS - LAG, NS):
                    pv(unit, 1, s)
                at = At(len(PREFETCH) + PAIRS * NF - 1, PER_BATCH, 0, b)
                norm(("norm", 1, 0), take_work(at, at.c), unit)
                pe.wait_ge(o_free, At((PAIRS - 1) * CHUNKS + CHUNKS + O_CREDIT, PAIRS * CHUNKS, 0, b).value())
                for half in range(CHUNKS):
                    at = at + 1
                    w = take_work(at, at.c)
                    for i in range(TPC):
                        tok = (half * TPC + i) * P
                        for pr in range(PAIRS):
                            t = nc.tensor.matmul(w[:, i * P:(i + 1) * P], OT[:, pr, tok:tok + P], WOT[:, pr, :],
                                                 start=pr == 0, stop=pr == PAIRS - 1)
                    t.then_inc(work_ready, 1)

            pe.wait_ge(xt_lo, B * CHUNKS)
            pe.wait_ge(consts_set, 3)
            for n, f in enumerate(PREFETCH):
                filler(f, At(n), At(-1), 0, 0)
            with pe.Fori(0, B) as b:
                for par in range(2):
                    window(b, None, par, par == 0)
                with pe.Fori(1, PAIRS // 2) as j:
                    for par in range(2):
                        window(b, j, par, False)
                flush(b)

            def up(g):
                for i in range(TPC):
                    pe.wait_ge(x1_made, g * TPC + i + 1)
                    if i == 0 and g >= 2:
                        pe.wait_ge(x1t_copied, g - 1)
                    t = nc.tensor.transpose(O[g % 2][:, i * P:(i + 1) * P], X[:, g * TPC + i, :], IDN[:])
                t.then_inc(x1t_made, 1)
                pe.wait_ge(x1t_copied, g + 1)
                for t_ in range(HT):
                    if g > 0:
                        pe.wait_ge(gelu_done, (g - 1) * HT + t_ + 1)
                    nc.tensor.matmul(banks[t_], W1[:, t_ * P:(t_ + 1) * P], x1T[g % 2], start=True,
                                     stop=True).then_inc(hid_ready, 1)

            def down(g):
                pe.wait_ge(gelu_done, (g + 1) * HT)
                if g >= 2:
                    pe.wait_ge(h2_made, g - 1)
                for i in range(TPC):
                    for t_ in range(HT):
                        t = nc.tensor.matmul(WORK[g % 2][:, i * P:(i + 1) * P], G[g % 2][:, t_, i * P:(i + 1) * P],
                                             W2[:, t_, :], start=t_ == 0, stop=t_ == HT - 1)
                t.then_inc(y_ready, 1)

            pe.wait_ge(stats_made, B * TILES)
            for g in range(B * CHUNKS):
                up(g)
                if g > 0:
                    down(g - 1)
            down(B * CHUNKS - 1)

        @block.scalar
        def _(act):
            def hi(dst, src):
                return nc.scalar.activation(dst, src, ACT.Copy)

            def stage_weights(col):
                w = hi(WST[:, 0, :, :], WQKV[:, :, bass.ds(col, P)])
                w.then_inc(weights_hi, 1)

            banks = [SC[0][:, 0, :], SC[0][:, 1, :], SC[1][:, 0, :], SC[1][:, 1, :]]
            for g in range(B * CHUNKS):
                act.wait_ge(xt_made, g + 1)
                hi(XTH[:, g * CH:(g + 1) * CH], banks[g % 4]).then_inc(xt_hi, 1)
            act.wait_ge(wq_scaled, 1)
            stage_weights(0)

            def evacuate(f, at, unit, nxt):
                w, free = WORK[at.c % 2], work_free[at.c % 2]
                if f[0] == "proj":
                    _, n, c = f
                    act.wait_ge(work_ready, (at + 1).value())
                    cols = slice(c * CH, (c + 1) * CH)
                    A, Bh = slice(0, K), slice(K, P)
                    if n == 2:
                        hi(VT[:, c, :], w[:, :]).then_inc(free, 1)
                        return
                    T1, T2 = (QH, QH) if n == 0 else (KHL, KH1)
                    hi(T1[A, nxt, 0, cols], w[A, :])
                    hi(T1[Bh, nxt, 1, cols], w[Bh, :])
                    if n == 0:
                        hi(QH[Bh, nxt, 0, cols], w[A, :])
                        hi(QH[A, nxt, 1, cols], w[Bh, :]).then_inc(qk_hi, 1)
                    else:
                        hi(KH1[A, nxt, 0, cols], w[A, :])
                        hi(KH1[Bh, nxt, 1, cols], w[Bh, :]).then_inc(qk_hi, 1)
                elif f[0] == "vt":
                    c = f[1]
                    act.wait_ge(work_ready, (at + 1).value())
                    if c == 0 and not (at.b is None):
                        act.wait_ge(pv_done, (unit.times(NS) + PV_CREDIT).value())
                    hi(VP[:, nxt, c * TPC:(c + 1) * TPC, :], w[:, :].rearrange("p (t k) -> p t k", t=TPC))\
                        .then_inc(free, 1)

            def exp(unit, s):
                qc, kt = STEPS[s]
                n = CH - START[s]
                act.wait_ge(scores_ready, (unit.times(NS) + (s + 1)).value())
                if kt == 0:
                    act.wait_ge(o_free, (unit.times(CHUNKS) + (qc + 1)).value())
                else:
                    act.wait_ge(pv_done, (unit.times(NS) + (s + 1 - PRING + PV_CREDIT)).value())
                    act.wait_ge(add_done, (unit.times(NA) + (adds_until(s + 1 - PRING) + ADD_CREDIT)).value())
                nc.scalar.activation(prob(s), SC[s % 2][:, :, 0:n], ACT.Exp).then_inc(exp_done, 1)

            def window(b, j, par, first):
                unit, base = unit_at(b, j, par), work_base(b, j, par)
                queue = fillers(first)
                for s in range(NS):
                    exp(unit, s)
                    for at, f, n in queue:
                        if at == s:
                            evacuate(f, base + n, unit, 1 - par)
                            if f == ("proj", 2, 1):
                                stage_weights(pair_col(j, par, 2))

            act.wait_ge(rows_set, 1)
            for n, f in enumerate(PREFETCH):
                evacuate(f, At(n), At(-1), 0)
                if f == ("proj", 2, 1):
                    stage_weights(P)
            with act.Fori(0, B) as b:
                for par in range(2):
                    window(b, None, par, par == 0)
                with act.Fori(1, PAIRS // 2) as j:
                    for par in range(2):
                        window(b, j, par, False)

            def deviation(n):
                act.wait_ge(var_ready, n)
                nc.scalar.activation(RSTD[:, :], MV[:, :, 1], ACT.Sqrt, bias=EPST[:, 0:1]).then_inc(std_made, 1)

            deviation(1)
            for g in range(B * CHUNKS):
                for t_ in range(HT):
                    act.wait_ge(hid_ready, g * HT + t_ + 1)
                    if t_ == 0 and g >= 2:
                        act.wait_ge(y_ready, g - 1)
                    nc.scalar.activation(G[g % 2][:, t_, :], banks[t_], ACT.Gelu,
                                         bias=BIAS1[:, t_:t_ + 1]).then_inc(gelu_done, 1)
            deviation(2)

        @block.vector
        def _(dve):
            links = [0]

            def link(op):
                links[0] += 1
                op.then_inc(dve_self, 1)
                dve.wait_ge(dve_self, links[0])

            def lo(dst, src, hi_part):
                return nc.vector.tensor_tensor(dst, src, hi_part.bitcast(F32), ALU.subtract)

            dve.wait_ge(in_w, 64)
            nc.vector.tensor_scalar(WQKV[:, 0, :], WQKV[:, 0, :], K ** -0.5, None, ALU.mult).then_inc(wq_scaled, 1)
            nc.vector.memset(KH1[K:P, :, 0, :].bitcast(F32), 0.0)
            nc.vector.memset(KH1[0:K, :, 1, :].bitcast(F32), 0.0)
            nc.vector.memset(QL[K:P, :, 0, :].bitcast(F32), 0.0)
            link(nc.vector.memset(QL[0:K, :, 1, :].bitcast(F32), 0.0))
            nc.vector.memset(KH1[K:K + 1, :, 0, :].bitcast(F32), 1.0)
            nc.vector.memset(KH1[0:1, :, 1, :].bitcast(F32), 1.0)
            nc.vector.memset(MP[:], LOWEST).then_inc(rows_set, 1)

            banks = [SC[0][:, 0, :], SC[0][:, 1, :], SC[1][:, 0, :], SC[1][:, 1, :]]
            for g in range(B * CHUNKS):
                dve.wait_ge(xt_hi, g + 1)
                lo(XTL[:, g * CH:(g + 1) * CH], banks[g % 4], XTH[:, g * CH:(g + 1) * CH]).then_inc(xt_lo, 1)
            for g in range(2):
                dve.wait_ge(wt_made, g + 1)
                nc.vector.tensor_copy(WOT[:, g * TPC:(g + 1) * TPC, :],
                                      O[g][:, :].rearrange("p (t d) -> p t d", t=TPC)).then_inc(wt_copied, 1)
            dve.wait_ge(w2t_made, 1)
            link(nc.vector.tensor_copy(w2t, O[0][:, :]))
            dve.wait_ge(in_mlp, 16 * 6)
            link(nc.vector.tensor_tensor(BC[:, :], BC[:, :], down_row, ALU.add))
            for n in range(2 * STAGES):
                dve.wait_ge(stage_in[n % WST_SLOTS], 16 * (n // WST_SLOTS + 1))
                is_up = n < STAGES
                target = W1[:, :] if is_up else w2t
                ops = butterfly_stage(nc.vector, target, fly_a, fly_b, stage_w[:, n % WST_SLOTS, :],
                                      n if is_up else 2 * STAGES - 1 - n, is_up)
                ops[0]()
                link(ops[1]())
                op = ops[2]()
                op.then_inc(stage_used, 1)
                dve.wait_ge(stage_used, n + 1)
            dve.sem_inc(wt_copied, 2)
            dve.wait_ge(w2_made, 1)
            nc.vector.tensor_copy(W2[:, :, :], O[1][:, :].rearrange("p (t d) -> p t d", t=HT)).then_inc(w2_copied, 1)
            dve.wait_ge(bias_made, 1)
            nc.vector.tensor_copy(BIAS1[:, :], O[0][:, 0:HT]).then_inc(w2_copied, 1)

            def stage_low(col, staged):
                dve.wait_ge(weights_hi, staged.value())
                lo(WST[:, 1, :, :], WQKV[:, :, bass.ds(col, P)], WST[:, 0, :, :]).then_inc(weights_lo, 1)

            stage_low(0, At(1))
            for cr, n in ((exp_done, EXP_CREDIT), (pv_done, PV_CREDIT), (o_free, O_CREDIT)):
                dve.sem_inc(cr, n)

            def consume(f, at, unit, nxt, pair=None):
                w = WORK[at.c % 2]
                free = work_free[at.c % 2]
                if f[0] == "proj" and f[1] < 2:
                    _, n, c = f
                    done = {(0, 0): 1, (1, 0): 2, (0, 1): 3, (1, 1): 4}[(n, c)]
                    dve.wait_ge(qk_hi, ((unit + 1).times(4) + done).value())
                    cols = slice(c * CH, (c + 1) * CH)
                    A, Bh = slice(0, K), slice(K, P)
                    if n == 0:
                        lo(QL[A, nxt, 0, cols], w[A, :], QH[A, nxt, 0, cols])
                        op = lo(QL[Bh, nxt, 1, cols], w[Bh, :], QH[Bh, nxt, 1, cols])
                    else:
                        lo(KHL[Bh, nxt, 0, cols], w[A, :], KHL[A, nxt, 0, cols])
                        op = lo(KHL[A, nxt, 1, cols], w[Bh, :], KHL[Bh, nxt, 1, cols])
                    op.then_inc(free, 1)
                elif f[0] == "max":
                    _, h, qt, part = f
                    _, n = keys_of(part, qt)
                    cell = MP[:, h * TILES + qt, part:part + 1]
                    dve.wait_ge(work_ready, (at + 1).value())
                    if (part + 1) * TPC > qt:
                        dve.sem_inc(dve_passed, 1)
                        nc.vector.tensor_tensor_reduce(w[:, 0:n], w[:, 0:n], CMASK[:, CH - n:], 1.0, LOWEST,
                                                       ALU.add, ALU.max, cell).then_inc(free, 1)
                    else:
                        nc.vector.tensor_reduce(cell, w[:, 0:n], AX_X, ALU.max).then_inc(free, 1)
                    if f == MAXES[-1]:
                        dve.wait_ge(free, (at.half() + 1).value())
                        nc.vector.tensor_reduce(NEGM[:, :], MP[:, :, :], AX_X, ALU.max,
                                                negate=True).then_inc(negm_made, 1)
                elif f[0] == "mt":
                    dve.wait_ge(work_ready, (at + 1).value())
                    if not (at.b is None):
                        dve.wait_ge(m_landed, (unit + 1).times(32).value())
                    nc.vector.tensor_copy(NROW[:, :], w[0:2 * TILES, 0:P]).then_inc(nrow_made, 1)
                    dve.wait_ge(nrow_made, (unit + 2).value())
                    dve.sem_inc(free, 1)
                elif f[0] == "norm":
                    _, qc, back = f
                    dve.wait_ge(work_ready, (at + 1).value())
                    nc.vector.reciprocal(R[:, :], w[:, :]).then_inc(free, 1)
                    dve.wait_ge(free, (at.half() + 1).value())
                    dst = OT[:, bass.ds(pair, 1), qc * CH:(qc + 1) * CH].rearrange("p a c -> p (a c)")
                    nc.vector.tensor_tensor(dst, O[qc][:, :], R[:, :], ALU.mult).then_inc(o_free, 1)

            def window(b, j, par, first):
                unit, base = unit_at(b, j, par), work_base(b, j, par)
                mine = par if j is None else j * 2 + par
                for s, f, n in fillers(first):
                    back = f[2] if f[0] == "norm" else 0
                    consume(f, base + n, unit, 1 - par, pair=mine - back)
                    if f == ("proj", 2, 1):
                        stage_low(pair_col(j, par, 2), unit + 3)

            dve.wait_ge(consts_set, 3)
            for n, f in enumerate(PREFETCH):
                consume(f, At(n), At(-1), 0)
                if f == ("proj", 2, 1):
                    stage_low(P, At(2))

            with dve.Fori(0, B) as b:
                for par in range(2):
                    window(b, None, par, par == 0)
                with dve.Fori(1, PAIRS // 2) as j:
                    for par in range(2):
                        window(b, j, par, False)
                at = At(len(PREFETCH) + PAIRS * NF - 1, PER_BATCH, 0, b)
                unit = At(PAIRS - 1, PAIRS, 0, b)
                consume(("norm", 1, 0), at, unit, 0, pair=PAIRS - 1)
                for half in range(CHUNKS):
                    at = at + 1
                    dve.wait_ge(work_ready, (at + 1).value())
                    xs = X[:, bass.ds(b * TILES + half * TPC, TPC), :]
                    nc.vector.tensor_tensor(xs, WORK[at.c % 2][:, :].rearrange("p (t d) -> p t d", t=TPC), xs,
                                            ALU.add).then_inc(work_free[at.c % 2], 1)
                    dve.wait_ge(work_free[at.c % 2], (at.half() + 1).value())
                    dve.sem_inc(dve_passed, 1)
                    for i in range(TPC):
                        nc.vector.bn_stats(BS[:, i, :], X[:, bass.ds(b * TILES + (half * TPC + i), 1), :]
                                           .rearrange("p a d -> p (a d)")).then_inc(h1_added, 1)
                    dve.wait_ge(h1_added, b * TILES + (half + 1) * TPC)
                    dve.sem_inc(dve_passed, 1)
                    for i in range(TPC):
                        nc.vector.bn_aggr(MVT[:, i, :], BS[:, i, :]).then_inc(aggregated, 1)
                    dve.wait_ge(aggregated, (b * TILES + (half + 1) * TPC))
                    nc.vector.tensor_copy(MV[:, bass.ds(b * TILES + half * TPC, TPC), :], MVT[:, :, :])\
                        .then_inc(stats_made, TPC)

            def rstd(n):
                dve.wait_ge(stats_made, n * B * TILES)
                dve.sem_inc(var_ready, 1)
                dve.wait_ge(std_made, n)
                link(nc.vector.reciprocal(RSTD[:, :], RSTD[:, :]))

            def normalise(t, done):
                nc.vector.tensor_scalar(X[:, t, :], X[:, t, :], MV[:, t, 0:1], RSTD[:, t:t + 1],
                                        ALU.subtract, ALU.mult).then_inc(done, 1)

            def residual(g):
                dve.wait_ge(y_ready, g + 1)
                xs = X[:, g * TPC:(g + 1) * TPC, :]
                nc.vector.tensor_tensor(xs, WORK[g % 2][:, :].rearrange("p (t d) -> p t d", t=TPC), xs,
                                        ALU.add).then_inc(h2_made, 1)
                dve.wait_ge(h2_made, g + 1)
                for i in range(TPC):
                    nc.vector.bn_stats(BS[:, i, :], X[:, g * TPC + i, :]).then_inc(h1_added, 1)
                dve.wait_ge(h1_added, (B * CHUNKS + g + 1) * TPC)
                for i in range(TPC):
                    nc.vector.bn_aggr(MV[:, g * TPC + i, :], BS[:, i, :]).then_inc(stats_made, 1)

            rstd(1)
            for i in range(TPC):
                normalise(i, x1_made)
            for g in range(B * CHUNKS):
                dve.wait_ge(x1t_made, g + 1)
                nc.vector.tensor_copy(x1T[g % 2], O[g % 2][:, :]).then_inc(x1t_copied, 1)
                if g + 1 < B * CHUNKS:
                    for i in range(TPC):
                        normalise((g + 1) * TPC + i, x1_made)
                for i in range(TPC):
                    t = g * TPC + i
                    op = nc.vector.tensor_tensor(X[:, t, :], X[:, t, :], BC[:, :], ALU.add)
                link(op)
                if g > 0:
                    residual(g - 1)
            residual(B * CHUNKS - 1)
            rstd(2)
            for t in range(B * TILES):
                normalise(t, out_made)


_INS = ["L0_attn_x_BSE", "L0_attn_w_q", "L0_attn_w_k", "L0_attn_w_v", "L0_attn_w_o", "L0_ffn_W_exp", "L0_ffn_b_exp",
        "L0_ffn_up_weights", "L0_ffn_up_bias", "L0_ffn_down_weights", "L0_ffn_W_con", "L0_ffn_b_con",
        "L0_ffn_down_bias"]
_OUTS = [((B, S, D), "float32")]


def kernel(**inputs):
    import numpy as _np
    import concourse.bacc as _bacc
    from concourse import mybir as _mybir
    from concourse.bass_utils import run_bass_kernel_spmd as _run

    nc = _bacc.Bacc("TRN2", target_bir_lowering=False, num_devices=1)
    arrays, args = {}, []
    for name in _INS:
        a = _np.ascontiguousarray(inputs[name])
        arrays[f"in_{name}_dram"] = a
        args.append(nc.dram_tensor(f"in_{name}_dram", a.shape, _mybir.dt.from_np(a.dtype), kind="ExternalInput").ap())
    for i, (shape, dtype) in enumerate(_OUTS):
        dt = _mybir.dt.from_np(_np.dtype(dtype))
        args.append(nc.dram_tensor(f"out_{i}_dram", shape, dt, kind="ExternalOutput").ap())
    post_norm_layer(nc, *args)
    r = _run(nc, [arrays], core_ids=[0])
    got = tuple(r.results[0][f"out_{i}_dram"] for i in range(len(_OUTS)))
    return got[0]
```

```python
from contextlib import ExitStack

import concourse.bass as bass
from concourse import mybir
from concourse.alu_op_type import AluOpType as ALU

ACT = mybir.ActivationFunctionType
F32 = mybir.dt.float32
F32R = mybir.dt.float32r
AX_X = mybir.AxisListType.X

P = 128
B, S, D = 4, 1024, 128
H, K = 16, 64
PAIRS = H // 2
UNITS = B * PAIRS
TILES = S // P
CH = 512
CHUNKS = S // CH
TPC = CH // P
HID = 512
HT = HID // P
STAGES = 9
BLOCK_STAGES = 7
AHEAD = 3
DOWN_LAG = 3
POOL_STAGES = 5
EPS = 1e-5
LOWEST = -3.0e38

STEPS = [(qc, kt) for qc in range(CHUNKS) for kt in range(TPC * (qc + 1))]
NS = len(STEPS)
START = [max(0, kt * P - qc * CH) for qc, kt in STEPS]
DIAG = [kt >= TPC * qc for qc, kt in STEPS]
ND = sum(DIAG)
ADDS = [kt > 0 for _, kt in STEPS]
NA = sum(ADDS)
LAG = 2
PRING = 3
LAST_OF = [max(s for s in range(NS) if STEPS[s][0] == qc) for qc in range(CHUNKS)]
FIRST_OF = [min(s for s in range(NS) if STEPS[s][0] == qc) for qc in range(CHUNKS)]


def diags_until(s):
    return sum(DIAG[:s])


def adds_until(s):
    return sum(ADDS[:s]) if s >= 0 else -sum(ADDS[s:])


MAXES = [("max", ((h, 0, 0), (h, 1, 0))) for h in range(2)]
MAXES += [("max", ((h, qt, 0),)) for qt in range(2, TPC) for h in range(2)]
CHUNK0_MAXES = len(MAXES)
MAXES += [("max", ((0, TPC, 1), (1, TPC, 1)))]
MAXES += [("max", ((h, qt, part),)) for qt in range(TPC, TILES) for part in range(2) for h in range(2)
          if (qt, part) != (TPC, 1)]
FILL = [[] for _ in range(NS)]
FILL[0] = [("proj", 1, 0), ("proj", 0, 1), ("proj", 2, 1)]
FILL[1] = [("proj", 1, 1), ("vt", 0)] + MAXES[0:1]
FILL[2] = [("norm", 1, 1)] + MAXES[1:2] + [("vt", 1)]
FILL[3] = MAXES[2:4]
FILL[4] = MAXES[4:6]
FILL[5] = MAXES[6:11]
FILL[6] = MAXES[11:16] + [("norm", 0, 0)] + MAXES[16:17]
FILL[7] = MAXES[17:19]
FILL[8] = MAXES[19:20]
FILL[9] = MAXES[20:21]
FILL[10] = [("mt",), ("proj", 0, 0), ("proj", 2, 0)]
FILL[11] = []
EARLY = [("proj", 0, 0), ("proj", 2, 0)]
LAST_PROJ = [f for fs in FILL for f in fs if f[0] == "proj" and f not in EARLY][-1]
assert sum(f[0] == "max" for fs in FILL for f in fs) == len(MAXES)
NWORK = 4
NF = sum(map(len, FILL))
PREFETCH = [(f, 1) for f in EARLY] + [(f, 1) for fs in FILL for f in fs if f[0] != "norm" and f not in EARLY]
PREFETCH += [(f, 2) for f in EARLY]
OUT_TILES = (2, 2, 2, 2)
assert sum(OUT_TILES) == TILES and all(TPC % n == 0 for n in OUT_TILES) and len(OUT_TILES) == NWORK and NF % NWORK == 0
PER_BATCH = PAIRS * NF + NWORK
NSC = 2
assert 2 * NS % NSC == 0


class At:

    def __init__(self, c, cb=0, cj=0, b=None, j=None):
        self.c, self.cb, self.cj, self.b, self.j = c, cb, cj, b, j

    def __add__(self, n):
        return At(self.c + n, self.cb, self.cj, self.b, self.j)

    def times(self, n):
        return At(self.c * n, self.cb * n, self.cj * n, self.b, self.j)

    def bank(self):
        assert self.cb % NWORK == 0 and self.cj % NWORK == 0
        return self.c % NWORK

    def uses(self):
        return At(self.c // NWORK, self.cb // NWORK, self.cj // NWORK, self.b, self.j)

    def value(self):
        v = 0
        if self.b is not None and self.cb:
            v = self.b * self.cb
        if self.j is not None and self.cj:
            v = self.j * self.cj + v
        v = v + self.c
        return v


def butterfly_op(eng, y, scratch, w, stage, rows, part):
    s, width = 2 ** stage, y.shape[-1]
    pairs = y.rearrange("p (n i s) -> p n s i", i=2, s=s)
    w = w.rearrange("p (n s o i) -> p n s o i", s=s, o=2, i=2)
    sides = [scratch[:, i * width:(i + 1) * width].rearrange("p (n s o) -> p n s o", s=s, o=2) for i in range(2)]
    if part == 2:
        return eng.tensor_tensor(pairs, sides[0], sides[1], ALU.add)
    src = pairs[:, :, :, part:part + 1].broadcast_to([y.shape[0], width // 2 // s, s, 2])
    wt = w[:, :, :, :, part] if rows else w[:, :, :, part, :]
    return eng.tensor_tensor(sides[part], src, wt, ALU.mult)


def post_norm_layer(nc, x, w_q, w_k, w_v, w_o, W_exp, b_exp, up_w, up_b, down_w, W_con, b_con, down_b, out):
    ctx = ExitStack()
    with ctx:
        def sb(name, shape, dt=F32):
            return ctx.enter_context(nc.sbuf_tensor(name, shape, dt))

        def sem(name):
            return ctx.enter_context(nc.semaphore(name))

        X = sb("X", [P, B * TILES, D])
        XTH = sb("XTH", [P, B * S], F32R)
        XTL = sb("XTL", [P, B * S], F32R)
        WQKV = sb("WQKV", [P, 3, H * K])
        WOT = sb("WOT", [P, PAIRS, D])
        OT = sb("OT", [P, PAIRS, S])
        QH = sb("QH", [P, 2, 2, S], F32R)
        QL = sb("QL", [P, 2, 2, S], F32R)
        KHL = sb("KHL", [P, 2, 2, S], F32R)
        KH1 = sb("KH1", [P, 2, 2, S], F32R)
        PR = sb("PR", [P, PRING, 2, CH])
        SUM = sb("SUM", [P, CHUNKS, 2, CH])
        VP = sb("VP", [P, 2, TILES, 2 * K])
        VT = sb("VT", [P, CHUNKS, CH])
        WST = sb("WST", [P, 2, 3, P], F32R)
        CMASK = sb("CMASK", [P, CH])
        IDN = sb("IDN", [P, P])
        ONES = sb("ONES", [P, K])
        R0 = sb("R0", [P, CH])
        R = sb("R", [P, CH])
        MP = sb("MP", [P, 2 * TILES, 2])
        NEGM = sb("NEGM", [P, 2 * TILES])
        NROW = sb("NROW", [2 * TILES, P], F32R)
        MV = sb("MV", [P, B * TILES, 2])
        MVT = sb("MVT", [P, TPC, 2])
        BS = sb("BS", [P, TPC, 6])
        RSTD = sb("RSTD", [P, B * TILES])
        HALF = sb("HALF", [P, B * TILES])
        W1 = sb("W1", [P, HID])
        W2 = sb("W2", [P, HT, D])
        BC = sb("BC", [P, D])
        BIAS1 = sb("BIAS1", [P, HT])

        inner_w = [OT[0:HT, st // 4, st % 4 * 2 * P:(st % 4 + 1) * 2 * P] for st in range(BLOCK_STAGES)]
        outer_w = [OT[0:1, 2 + i, :] for i in range(STAGES - BLOCK_STAGES)]
        BLOCKS = R[0:HT, 0:P]
        w_raw = PR[:, :, :, :].rearrange("p a h c -> p (a h c)")
        wo_nat = w_raw[:, 0:1024]
        wcon_nat = w_raw[:, 1024:1536].rearrange("p (t d) -> p t d", t=HT)
        up_b_row = w_raw[0:1, 2048:2048 + HID]
        fly = SUM[:, :, :, :].rearrange("p a h c -> p (a h c)")
        block_scratch, row_scratch = fly[0:HT, 0:2 * P], fly[0:1, 0:2 * HID]
        down_row = w_raw[:, 2560:2560 + D]
        BROW = R0[0:1, :]
        late = [WQKV[:, i, :] for i in range(3)] + [VT[:, :, :].rearrange("p c n -> p (c n)")]
        up_w_slot = [late[n % 4] for n in range(STAGES)]
        up_scratch = VP[:, 0].rearrange("p t k -> p (t k)")
        down_w_slot = [VP[:, 1].rearrange("p t k -> p (t k)")] + [PR[:, i].rearrange("p h c -> p (h c)") for i in range(PRING)]
        down_w_slot += late + [up_scratch]
        assert len(down_w_slot) == STAGES
        down_scratch = SUM[:, 0].rearrange("p h c -> p (h c)")
        w2t = W2[:, :, :].rearrange("p t d -> p (t d)")
        ot_flat = OT[:, :, :].rearrange("p a s -> p (a s)")
        x1T = [CMASK[:, :], SUM[:, 1, 0, :]]
        G = [ot_flat[:, HT * i * CH:HT * (i + 1) * CH].rearrange("p (t c) -> p t c", t=HT)
             for i in range(DOWN_LAG + 1)]

        SC = [ctx.enter_context(nc.psum_tensor(f"SC{i}", [P, CH], F32)) for i in range(NSC)]
        O = [ctx.enter_context(nc.psum_tensor(f"O{i}", [P, CH], F32)) for i in range(2)]
        WORK = [ctx.enter_context(nc.psum_tensor(f"WORK{i}", [P, CH], F32)) for i in range(NWORK)]

        in_x, in_w = [sem("in_x0"), sem("in_x1")], sem("in_w")
        in_exp, in_wo, in_con, in_b, in_bc = sem("in_exp"), sem("in_wo"), sem("in_con"), sem("in_b"), sem("in_bc")
        in_rows, blocks_done, brow_in = sem("in_rows"), sem("blocks_done"), sem("brow_in")
        up_in, down_in = [[sem(f"{w}_in{i}") for i in range(STAGES)] for w in ("up", "down")]
        up_done, down_done = sem("up_done"), sem("down_done")
        consts_set = sem("consts_set")
        rows_set, ones_rows_set, bc_made = sem("rows_set"), sem("ones_rows_set"), sem("bc_made")
        idn_set = sem("idn_set")
        pool_passed, dve_passed = sem("pool_passed"), sem("dve_passed")
        pool_self, dve_self = sem("pool_self"), sem("dve_self")
        laid_made, laid_copied, xt_hi = sem("laid_made"), sem("laid_copied"), sem("xt_hi")
        half_set, eps_added = sem("half_set"), sem("eps_added")
        brow_made, rstd_made, w2_made, w2_copied = sem("brow_made"), sem("rstd_made"), sem("w2_made"), sem("w2_copied")
        weights_hi, weights_lo = sem("weights_hi"), sem("weights_lo")
        work_ready = sem("work_ready")
        work_free = [sem(f"work_free{i}") for i in range(NWORK)]
        qk_hi = sem("qk_hi")
        dup_landed = [sem("dup_landed0"), sem("dup_landed1")]
        ln_made, recip_made, inverse_made = sem("ln_made"), sem("recip_made"), sem("inverse_made")
        negm_made, nrow_made, m_landed = sem("negm_made"), sem("nrow_made"), sem("m_landed")
        scores_ready, exp_done, mask_done = sem("scores_ready"), sem("exp_done"), sem("mask_done")
        pv_done, add_done, o_free = sem("pv_done"), sem("add_done"), sem("o_free")
        h1_added, stats_made = sem("h1_added"), sem("stats_made")
        aggregated = sem("aggregated")
        x1_made, x1t_made, x1t_copied = sem("x1_made"), sem("x1t_made"), sem("x1t_copied")
        hid_ready, gelu_done, y_ready, h2_made = sem("hid_ready"), sem("gelu_done"), sem("y_ready"), sem("h2_made")
        out_made, out_stored = sem("out_made"), sem("out_stored")

        EXP_CREDIT, PV_CREDIT, ADD_CREDIT, O_CREDIT = NSC, PRING, PRING, 2

        LAY = [("x", g) for g in range(B * CHUNKS)] + [("wo", g) for g in range(CHUNKS)] + [("con", 0)]

        def lays_after(n):
            return [CHUNKS + (n - 8) // 2] if n >= 8 and n % 2 == 0 and CHUNKS + (n - 8) // 2 < len(LAY) else []

        assert CHUNKS + (len(PREFETCH) - 9) // 2 >= len(LAY)
        lay_banks = [SC[0][:, :], SC[1][:, :], O[0][:, :], O[1][:, :]]
        hid_banks = [SC[0][:, :], SC[1][:, :], WORK[2][:, :], WORK[3][:, :]]

        x_tiles = x.rearrange("b (t p) d -> p (b t) d", p=P)
        out_tiles = out.rearrange("b (t p) d -> p (b t) d", p=P)

        def unit_at(b, j, par):
            return At(par, PAIRS, 2, b, j)

        FIRST, MIDDLE, PENULTIMATE, LAST = range(4)

        def sweep(eng, window, flush):
            with eng.Fori(0, B - 1) as b:
                window(b, None, 0, FIRST)
                window(b, None, 1, MIDDLE)
                with eng.Fori(1, PAIRS // 2) as j:
                    window(b, j, 0, MIDDLE)
                    window(b, j, 1, MIDDLE)
                flush(b)
            window(B - 1, None, 0, FIRST)
            window(B - 1, None, 1, MIDDLE)
            with eng.Fori(1, PAIRS // 2 - 1) as j:
                window(B - 1, j, 0, MIDDLE)
                window(B - 1, j, 1, MIDDLE)
            window(B - 1, PAIRS // 2 - 1, 0, PENULTIMATE)
            window(B - 1, PAIRS // 2 - 1, 1, LAST)
            flush(B - 1)

        def work_base(b, j, par, kind):
            return At(len(PREFETCH) + NF * par - (kind != FIRST) - (len(EARLY) if kind == LAST else 0),
                      PER_BATCH, 2 * NF, b, j)

        def flush_base(b):
            is_last = isinstance(b, int) and b == B - 1
            left_out = sum(NF - len(fillers(kind)) for kind in (PENULTIMATE, LAST)) if is_last else 0
            return At(len(PREFETCH) + PAIRS * NF - 1 - left_out, PER_BATCH, 0, b)

        def fillers(kind):
            n, made = 0, []
            for s, fs in enumerate(FILL):
                for f in fs:
                    if kind == FIRST and f == ("norm", 1, 1):
                        continue
                    if (kind == PENULTIMATE and f in EARLY) or (kind == LAST and f[0] != "norm"):
                        continue
                    made.append((s, f, n, 1 + (f in EARLY)))
                    n += 1
            return made

        def tokens_of(b, j, par, ahead):
            if j is None:
                return b * S
            if par + ahead < 2:
                return b * S
            return ((b * PAIRS + j * 2 + (par + ahead)) // PAIRS % B) * S

        def pair_col(j, par, ahead):
            if j is None:
                return (par + ahead) % PAIRS * P
            return ((j * 2 + (par + ahead)) % PAIRS) * P

        def keys_of(part, qt):
            lo = part * CH
            return lo, min(CH, (qt + 1) * P - lo)

        def prob(s, n=None):
            qc, kt = STEPS[s]
            n = CH - START[s] if n is None else n
            return SUM[:, qc, :, 0:n] if kt == 0 else PR[:, s % PRING, :, 0:n]

        block = ctx.enter_context(nc.Block())

        @block.sync
        def _(sp):
            sp.dma_start(X[:, 0:TILES, :], x_tiles[:, 0:TILES, :]).then_inc(in_x[0], 16)
            for n, w in enumerate((w_q, w_k, w_v)):
                sp.dma_start(WQKV[:, n, :], w.rearrange("e h k -> e (h k)")).then_inc(in_w, 16)
            sp.dma_start(BLOCKS, b_exp.rearrange("(a n) -> a n", a=HT)).then_inc(in_b, 16)
            sp.dma_start(up_b_row, up_b.rearrange("(a n) -> a n", a=1)).then_inc(in_b, 16)
            sp.dma_start(W1[:, :], W_exp).then_inc(in_exp, 16)

            def stage_weights(w, st, dst, done):
                src = w[st:st + 1].rearrange("a k i o -> a (k i o)").broadcast_to([P, 2 * HID])
                sp.dma_start(dst, src).then_inc(done, 16)

            for st in range(STAGES):
                w = up_w[st:st + 1].rearrange("s k i o -> s (k i o)")
                if st < BLOCK_STAGES:
                    sp.dma_start(inner_w[st], w.rearrange("s (a n) -> (s a) n", a=HT)).then_inc(in_rows, 16)
                else:
                    sp.dma_start(outer_w[st - BLOCK_STAGES], w).then_inc(in_rows, 16)
            sp.dma_start(X[:, TILES:, :], x_tiles[:, TILES:, :]).then_inc(in_x[1], 16)

            def copies(par, f_unit):
                A, Bh = slice(0, K), slice(K, P)
                for c in range(CHUNKS):
                    cols = slice(c * CH, (c + 1) * CH)
                    sp.wait_ge(qk_hi, (f_unit.times(2 * CHUNKS) + (2 * c + 1)).value())
                    for h, src, dst in ((0, A, Bh), (1, Bh, A)):
                        sp.dma_start(QH[dst, par, h, cols].bitcast(F32), QH[src, par, h, cols].bitcast(F32))\
                            .then_inc(dup_landed[c], 16)
                    sp.wait_ge(qk_hi, (f_unit.times(2 * CHUNKS) + (2 * c + 2)).value())
                    for h, half in ((0, A), (1, Bh)):
                        sp.dma_start(KH1[half, par, h, cols].bitcast(F32), KHL[half, par, h, cols].bitcast(F32))\
                            .then_inc(dup_landed[c], 16)

            def rows(par, f_unit):
                sp.wait_ge(nrow_made, (f_unit + 1).value())
                for h in range(2):
                    row = K if h == 0 else 0
                    dst = QL[row:row + 1, par, h, :].rearrange("a (t c) -> a t c", t=TILES)
                    sp.dma_start(dst.bitcast(F32), NROW[h * TILES:(h + 1) * TILES, :].bitcast(F32)).then_inc(m_landed, 16)

            copies(0, At(0))
            sp.wait_ge(blocks_done, 1)
            sp.dma_start(BROW, BLOCKS).then_inc(brow_in, 16)
            sp.dma_start(wo_nat, w_o.rearrange("e h k -> e (h k)")).then_inc(in_wo, 16)
            sp.dma_start(wcon_nat, W_con.rearrange("(t p) d -> p t d", p=P)).then_inc(in_con, 16)
            sp.dma_start(BC[:, :], b_con.rearrange("(a n) -> a n", a=1).broadcast_to([P, D])).then_inc(in_bc, 16)
            sp.dma_start(down_row, down_b.rearrange("(a n) -> a n", a=1).broadcast_to([P, D])).then_inc(in_bc, 16)
            rows(0, At(0))
            def window(b, j, par, kind):
                if kind != LAST:
                    unit = unit_at(b, j, par) + 1
                    copies(1 - par, unit)
                    rows(1 - par, unit)

            sweep(sp, window, lambda b: None)
            sp.wait_ge(m_landed, 32 * UNITS)
            for c in range(CHUNKS):
                sp.wait_ge(dup_landed[c], 64 * UNITS)
            sp.wait_ge(weights_lo, UNITS)
            for n in range(STAGES):
                if n >= 4:
                    sp.wait_ge(up_done, 3 * (n - 3))
                stage_weights(up_w, n, up_w_slot[n], up_in[n])
            sp.wait_ge(pv_done, NS * UNITS + PV_CREDIT)
            sp.wait_ge(add_done, NA * UNITS + ADD_CREDIT)
            for n in range(STAGES):
                if n == 1 + PRING:
                    sp.wait_ge(up_done, 3 * STAGES)
                stage_weights(down_w, STAGES - 1 - n, down_w_slot[n], down_in[n])
            for g in range(B * CHUNKS):
                sp.wait_ge(out_made, (g + 1) * TPC)
                sp.dma_start(out_tiles[:, g * TPC:(g + 1) * TPC, :],
                             X[:, g * TPC:(g + 1) * TPC, :]).then_inc(out_stored, 16)
            sp.wait_ge(out_stored, 16 * B * CHUNKS)

        @block.gpsimd
        def _(pool):
            nc.gpsimd.memset(IDN[:], 0.0).then_inc(pool_self, 1)
            nc.gpsimd.memset(CMASK[:], 0.0).then_inc(pool_self, 1)
            pool.wait_ge(pool_self, 1)
            nc.gpsimd.affine_select(out=IDN[:], in_=IDN[:], compare_op=ALU.not_equal, fill=1.0, base=0,
                                    pattern=[[-1, P]], channel_multiplier=1).then_inc(idn_set, 1)
            pool.wait_ge(pool_self, 2)
            nc.gpsimd.affine_select(out=CMASK[:, CH - P:], in_=CMASK[:, CH - P:], compare_op=ALU.is_ge, fill=LOWEST,
                                    base=0, pattern=[[-1, P]], channel_multiplier=1).then_inc(consts_set, 1)
            nc.gpsimd.memset(ONES[:], 1.0).then_inc(consts_set, 1)
            nc.gpsimd.memset(HALF[:], -0.5).then_inc(half_set, 1)
            pool.wait_ge(half_set, 1)
            nc.gpsimd.memset(KH1[K:P, :, 0, :].bitcast(F32), 1.0).then_inc(ones_rows_set, 1)
            pool.wait_ge(ones_rows_set, 1)
            nc.gpsimd.memset(KH1[0:K, :, 1, :].bitcast(F32), 1.0).then_inc(ones_rows_set, 1)
            pool.wait_ge(ones_rows_set, 2)
            pool.sem_inc(add_done, ADD_CREDIT)
            pool_n = 2
            pool.wait_ge(in_b, 32)
            pool.wait_ge(in_rows, 16 * STAGES)
            for st in range(STAGES):
                y, scratch, w = (BLOCKS, block_scratch, inner_w[st]) if st < BLOCK_STAGES else \
                    (BROW, row_scratch, outer_w[st - BLOCK_STAGES])
                if st == BLOCK_STAGES:
                    pool.sem_inc(blocks_done, 1)
                    pool.wait_ge(brow_in, 16)
                for part in range(3):
                    butterfly_op(nc.gpsimd, y, scratch, w, st, True, part).then_inc(pool_self, 1)
                    pool_n += 1
                    if part > 0:
                        pool.wait_ge(pool_self, pool_n)
            nc.gpsimd.tensor_tensor(BROW[:, :], BROW[:, :], up_b_row, ALU.add).then_inc(brow_made, 1)

            fill = nc.gpsimd.to_reg(0.0)

            def mask(unit, s):
                if not DIAG[s]:
                    return
                pool.wait_ge(exp_done, (unit.times(2 * NS) + (2 * s + 2 + EXP_CREDIT)).value())
                pool.sem_inc(pool_passed, 1)
                tri = prob(s, P)
                nc.gpsimd.affine_select(out=tri, in_=tri, compare_op=ALU.is_ge, fill=fill, base=0,
                                        pattern=[[0, 2], [1, P]], channel_multiplier=-1).then_inc(mask_done, 1)

            def add(unit, s):
                if not ADDS[s]:
                    return
                qc = STEPS[s][0]
                if DIAG[s]:
                    pool.wait_ge(mask_done, (unit.times(ND) + diags_until(s + 1)).value())
                else:
                    pool.wait_ge(exp_done, (unit.times(2 * NS) + (2 * s + 2 + EXP_CREDIT)).value())
                pool.wait_ge(pv_done, (unit.times(NS) + (FIRST_OF[qc] + 1 + PV_CREDIT)).value())
                pool.wait_ge(add_done, (unit.times(NA) + (adds_until(s) + ADD_CREDIT)).value())
                total = SUM[:, qc, :, START[s]:]
                nc.gpsimd.tensor_tensor(total, total, prob(s), ALU.add).then_inc(add_done, 1)

            def window(b, j, par, kind):
                unit = unit_at(b, j, par)
                for s in range(NS):
                    mask(unit, s)
                    if s > 0:
                        add(unit, s - 1)
                add(unit, NS - 1)

            sweep(pool, window, lambda b: None)

            deviations = [0]

            def deviation(lo, hi):
                rs = RSTD[:, lo:hi]
                nc.gpsimd.tensor_scalar(rs, MV[:, lo:hi, 1], EPS, None, ALU.add).then_inc(eps_added, 1)
                deviations[0] += 1
                pool.wait_ge(eps_added, deviations[0])
                nc.gpsimd.tensor_tensor(rs, rs, HALF[:, 0:hi - lo], ALU.pow).then_inc(rstd_made, 1)

            pool.wait_ge(pv_done, NS * UNITS + PV_CREDIT)
            for n in range(POOL_STAGES):
                if n == 0:
                    pool.wait_ge(half_set, 1)
                    pool.wait_ge(stats_made, (B - 1) * TILES)
                    deviation(0, AHEAD * TPC)
                pool.wait_ge(down_in[n], 16)
                for part in range(3):
                    butterfly_op(nc.gpsimd, w2t, down_scratch, down_w_slot[n], STAGES - 1 - n, False, part)\
                        .then_inc(down_done, 1)
                    if part > 0:
                        pool.wait_ge(down_done, 3 * n + part + 1)
            pool.wait_ge(stats_made, B * TILES)
            deviation(AHEAD * TPC, B * TILES)
            for g in range(B * CHUNKS):
                pool.wait_ge(x1_made, (g + 1) * TPC)
                pool.wait_ge(stats_made, (B * CHUNKS + g + 1) * TPC)
                deviation(g * TPC, (g + 1) * TPC)

        @block.tensor
        def _(pe):
            def lay(n):
                what, g = LAY[n]
                if what == "x":
                    pe.wait_ge(in_x[g >= CHUNKS], 16)
                    tiles = [X[:, g * TPC + i, :] for i in range(TPC)]
                elif what == "wo":
                    pe.wait_ge(in_wo, 16)
                    tiles = [wo_nat[:, (g * TPC + i) * P:(g * TPC + i + 1) * P] for i in range(TPC)]
                else:
                    pe.wait_ge(in_con, 16)
                    tiles = [wcon_nat[:, i, :] for i in range(HT)]
                if n >= 4:
                    pe.wait_ge(laid_copied, n - 3)
                for i, tile in enumerate(tiles):
                    t = nc.tensor.transpose(lay_banks[n % 4][:, i * P:(i + 1) * P], tile, IDN[:])
                t.then_inc(laid_made, 1)

            pe.wait_ge(idn_set, 1)
            for n in range(CHUNKS):
                lay(n)

            def take_work(at):
                if not (at.b is None and at.c < NWORK):
                    pe.wait_ge(work_free[at.bank()], at.uses().value())
                return WORK[at.bank()]

            def evacuated(at):
                pe.wait_ge(work_free[at.bank()], (at.uses() + 1).value())

            def filler(f, at, unit, nxt, tokens, numbers):
                w = take_work(at)
                if f[0] == "proj":
                    _, n, c = f
                    if f == ("proj", 0, 0):
                        pe.wait_ge(weights_lo, (unit + 2).value())
                    cols = bass.ds(tokens + c * CH, CH)
                    nc.tensor.matmul(w[:, :], WST[:, 0, n, :], XTH[:, cols], start=True, stop=False)
                    nc.tensor.matmul(w[:, :], WST[:, 1, n, :], XTH[:, cols], start=False, stop=False)
                    t = nc.tensor.matmul(w[:, :], WST[:, 0, n, :], XTL[:, cols], start=False, stop=True)
                elif f[0] == "vt":
                    c = f[1]
                    evacuated(numbers[("proj", 2 if c else 1, c)])
                    for i in range(TPC):
                        t = nc.tensor.transpose(w[:, i * P:(i + 1) * P], VT[:, c, i * P:(i + 1) * P], IDN[:])
                elif f[0] == "max":
                    pieces = f[1]
                    for c in range(CHUNKS):
                        if f == MAXES[c * CHUNK0_MAXES]:
                            if c > 0:
                                evacuated(numbers[("proj", 0, c)])
                            evacuated(numbers[("proj", 1, c)])
                            pe.wait_ge(dup_landed[c], (unit + 2).times(64).value())
                    at_col = 0
                    for h, qt, part in pieces:
                        lo, n = keys_of(part, qt)
                        t = nc.tensor.matmul(w[:, at_col:at_col + n], QH[:, nxt, h, qt * P:(qt + 1) * P],
                                             KHL[:, nxt, h, lo:lo + n], start=True, stop=True)
                        at_col += n
                elif f[0] == "mt":
                    pe.wait_ge(negm_made, (unit + 2).value())
                    t = nc.tensor.transpose(w[0:2 * TILES, 0:P], NEGM[:, :], IDN[:])
                else:
                    norm(f, w, unit)
                    return
                t.then_inc(work_ready, 1)

            def norm(f, w, unit):
                _, qc, before = f
                pe.wait_ge(add_done, ((unit + -before).times(NA) + (adds_until(LAST_OF[qc] + 1) + ADD_CREDIT)).value())
                for h in range(2):
                    t = nc.tensor.matmul(w[h * K:(h + 1) * K, :], ONES[:, :], SUM[:, qc, h, :], start=True, stop=True)
                t.then_inc(work_ready, 1)

            def scores(unit, par, s, between):
                qc, kt = STEPS[s]
                q0, n = qc * CH + START[s], CH - START[s]
                for h in range(2):
                    use = 2 * s + h
                    dst = SC[use % NSC][:, 0:n]
                    pe.wait_ge(exp_done, (unit.times(2 * NS) + (use + 1)).value())
                    nc.tensor.matmul(dst, KHL[:, par, h, kt * P:(kt + 1) * P], QH[:, par, h, q0:q0 + n],
                                     start=True, stop=False)
                    if s == 0 and h == 0:
                        pe.wait_ge(m_landed, ((unit + 1).times(32)).value())
                    nc.tensor.matmul(dst, KH1[:, par, h, kt * P:(kt + 1) * P], QL[:, par, h, q0:q0 + n],
                                     start=False, stop=True).then_inc(scores_ready, 1)
                    if h == 0:
                        between()

            def pv(unit, par, s):
                qc, kt = STEPS[s]
                n = CH - START[s]
                if kt == 0:
                    pe.wait_ge(o_free, (unit.times(CHUNKS) + (qc + 1)).value())
                if DIAG[s]:
                    pe.wait_ge(mask_done, (unit.times(ND) + diags_until(s + 1)).value())
                else:
                    pe.wait_ge(exp_done, (unit.times(2 * NS) + (2 * s + 2 + EXP_CREDIT)).value())
                p = prob(s)
                for h in range(2):
                    t = nc.tensor.matmul(O[qc][h * K:(h + 1) * K, START[s]:], VP[:, par, kt, h * K:(h + 1) * K],
                                         p[:, h, :], start=kt == 0, stop=s == LAST_OF[qc])
                t.then_inc(pv_done, 1)

            def window(b, j, par, kind):
                unit, base = unit_at(b, j, par), work_base(b, j, par, kind)
                queue = fillers(kind)
                numbers = {f: base + n for _, f, n, _ in queue}
                for s in range(NS):
                    mine = [(f, n, ahead) for at, f, n, ahead in queue if at == s]

                    def fill(k):
                        for f, n, ahead in mine[:k]:
                            filler(f, base + n, unit + (ahead - 1), (par + ahead) % 2, tokens_of(b, j, par, ahead), numbers)
                        del mine[:k]

                    def fill_one():
                        if mine and not (s < LAG and mine[0][0] == ("norm", 1, 1)):
                            fill(1)

                    scores(unit, par, s, fill_one)
                    fill_one()
                    if s >= LAG:
                        pv(unit, par, s - LAG)
                    elif kind != FIRST:
                        pv(unit + -1, 1 - par, NS + s - LAG)
                    fill(len(mine))

            def flush(b):
                unit = At(PAIRS - 1, PAIRS, 0, b)
                for s in range(NS - LAG, NS):
                    pv(unit, 1, s)
                at = flush_base(b)
                tile = 0
                for n, tiles in enumerate(OUT_TILES):
                    if n == 1:
                        norm(("norm", 1, 0), take_work(at), unit)
                        at = at + 1
                    pe.wait_ge(o_free, At((PAIRS - 1) * CHUNKS + tile // TPC + 1 + O_CREDIT, PAIRS * CHUNKS, 0, b).value())
                    w = take_work(at)
                    for i in range(tiles):
                        tok = (tile + i) * P
                        for pr in range(PAIRS):
                            t = nc.tensor.matmul(w[:, i * P:(i + 1) * P], OT[:, pr, tok:tok + P], WOT[:, pr, :],
                                                 start=pr == 0, stop=pr == PAIRS - 1)
                    t.then_inc(work_ready, 1)
                    tile += tiles
                    at = at + 1

            pe.wait_ge(laid_copied, CHUNKS)
            for n, (f, ahead) in enumerate(PREFETCH):
                filler(f, At(n), At(ahead - 2), ahead - 1, 0, {g: At(m) for m, (g, a) in enumerate(PREFETCH) if a == 1})
                for job in lays_after(n):
                    lay(job)
            pe.wait_ge(consts_set, 2)
            pe.wait_ge(brow_made, 1)
            pe.wait_ge(laid_copied, len(LAY) - 3)
            for i in range(HT):
                t = nc.tensor.matmul(lay_banks[len(LAY) % 4][:, i:i + 1], BROW[:, i * P:(i + 1) * P], ONES[0:1, 0:1],
                                     start=True, stop=True)
            t.then_inc(laid_made, 1)
            pe.wait_ge(ones_rows_set, 2)
            pe.wait_ge(laid_copied, len(LAY) + 1)
            sweep(pe, window, flush)

            def transpose_x1(g):
                for i in range(TPC):
                    pe.wait_ge(x1_made, g * TPC + i + 1)
                    if i == 0 and g >= 2:
                        pe.wait_ge(x1t_copied, g - 1)
                    t = nc.tensor.transpose(O[g % 2][:, i * P:(i + 1) * P], X[:, g * TPC + i, :], IDN[:])
                t.then_inc(x1t_made, 1)

            def up(g):
                pe.wait_ge(x1t_copied, g + 1)
                for t_ in range(HT):
                    if g > 0:
                        pe.wait_ge(gelu_done, (g - 1) * HT + t_ + 1)
                    nc.tensor.matmul(hid_banks[t_], W1[:, t_ * P:(t_ + 1) * P], x1T[g % 2], start=True,
                                     stop=True).then_inc(hid_ready, 1)

            def down(g):
                pe.wait_ge(gelu_done, (g + 1) * HT)
                if g >= 2:
                    pe.wait_ge(h2_made, g - 1)
                for i in range(TPC):
                    for t_ in range(HT):
                        t = nc.tensor.matmul(WORK[g % 2][:, i * P:(i + 1) * P], G[g % (DOWN_LAG + 1)][:, t_, i * P:(i + 1) * P],
                                             W2[:, t_, :], start=t_ == 0, stop=t_ == HT - 1)
                t.then_inc(y_ready, 1)

            pe.wait_ge(o_free, CHUNKS * UNITS + O_CREDIT)
            transpose_x1(0)
            transpose_x1(1)
            for n in range(1, NWORK + 1):
                evacuated(flush_base(B - 1) + n)
            for g in range(B * CHUNKS):
                up(g)
                if g + 2 < B * CHUNKS:
                    transpose_x1(g + 2)
                if g == DOWN_LAG:
                    pe.wait_ge(down_done, 3 * STAGES)
                    for i in range(HT):
                        t = nc.tensor.transpose(WORK[1][:, i * P:(i + 1) * P], w2t[:, i * P:(i + 1) * P], IDN[:])
                    t.then_inc(w2_made, 1)
                    pe.wait_ge(w2_copied, 1)
                if g >= DOWN_LAG:
                    down(g - DOWN_LAG)
            for g in range(B * CHUNKS - DOWN_LAG, B * CHUNKS):
                down(g)

        @block.scalar
        def _(act):
            def hi(dst, src):
                return nc.scalar.activation(dst, src, ACT.Copy)

            def stage_weights(col):
                w = hi(WST[:, 0, :, :], WQKV[:, :, bass.ds(col, P)])
                w.then_inc(weights_hi, 1)

            nc.scalar.preload_act_table_set("natural_log_exp_and_others")
            def lay(n):
                act.wait_ge(laid_made, n + 1)
                hi(XTH[:, n * CH:(n + 1) * CH], lay_banks[n % 4]).then_inc(xt_hi, 1)

            for n in range(CHUNKS):
                lay(n)
            act.wait_ge(in_w, 48)
            stage_weights(0)

            def evacuate(f, at, unit, nxt):
                w, free = WORK[at.bank()], work_free[at.bank()]
                if f[0] == "proj":
                    _, n, c = f
                    act.wait_ge(work_ready, (at + 1).value())
                    cols = slice(c * CH, (c + 1) * CH)
                    A, Bh = slice(0, K), slice(K, P)
                    if n == 2:
                        hi(VT[:, c, :], w[:, :]).then_inc(free, 1)
                        return
                    T = QH if n == 0 else KHL
                    hi(T[A, nxt, 0, cols], w[A, :])
                    hi(T[Bh, nxt, 1, cols], w[Bh, :]).then_inc(qk_hi, 1)
                elif f[0] == "vt":
                    c = f[1]
                    act.wait_ge(work_ready, (at + 1).value())
                    if c == 0 and not (at.b is None):
                        act.wait_ge(pv_done, (unit.times(NS) + PV_CREDIT).value())
                    hi(VP[:, nxt, c * TPC:(c + 1) * TPC, :], w[:, :].rearrange("p (t k) -> p t k", t=TPC))\
                        .then_inc(free, 1)
                elif f[0] == "norm":
                    _, qc, back = f
                    norms = (unit + -back).times(CHUNKS) + qc
                    act.wait_ge(work_ready, (at + 1).value())
                    act.wait_ge(o_free, (norms + O_CREDIT).value())
                    nc.scalar.activation(R0[:, :], w[:, :], ACT.Ln).then_inc(ln_made, 1)
                    act.wait_ge(ln_made, (norms + 1).value())
                    nc.scalar.activation(R0[:, :], R0[:, :], ACT.Exp, scale=-1.0).then_inc(recip_made, 1)

            def exp(unit, s, h):
                qc, kt = STEPS[s]
                n, use = CH - START[s], 2 * s + h
                act.wait_ge(scores_ready, (unit.times(2 * NS) + (use + 1)).value())
                if h == 0 and kt == 0:
                    act.wait_ge(o_free, (unit.times(CHUNKS) + (qc + 1)).value())
                elif h == 0:
                    act.wait_ge(pv_done, (unit.times(NS) + (s + 1 - PRING + PV_CREDIT)).value())
                    act.wait_ge(add_done, (unit.times(NA) + (adds_until(s + 1 - PRING) + ADD_CREDIT)).value())
                nc.scalar.activation(prob(s)[:, h, :], SC[use % NSC][:, 0:n], ACT.Exp,
                                     scale=K ** -0.5).then_inc(exp_done, 1)

            def window(b, j, par, kind):
                unit, base = unit_at(b, j, par), work_base(b, j, par, kind)
                queue = fillers(kind)
                for s in range(NS):
                    exp(unit, s, 0)
                    mine = [(f, n, ahead) for at, f, n, ahead in queue if at == s]
                    for i, (f, n, ahead) in enumerate(mine):
                        evacuate(f, base + n, unit, (par + ahead) % 2)
                        if f == LAST_PROJ and kind in (FIRST, MIDDLE):
                            stage_weights(pair_col(j, par, 2))
                        if i == 0:
                            exp(unit, s, 1)
                    if not mine:
                        exp(unit, s, 1)

            act.wait_ge(rows_set, 1)
            for n, (f, ahead) in enumerate(PREFETCH):
                evacuate(f, At(n), At(-1), ahead - 1)
                for job in lays_after(n):
                    if LAY[job][0] == "x":
                        lay(job)
                if f == LAST_PROJ:
                    stage_weights(P)

            def flush(b):
                evacuate(("norm", 1, 0), flush_base(b) + 1, At(PAIRS - 1, PAIRS, 0, b), 0)

            sweep(act, window, flush)

            for g in range(B * CHUNKS):
                for t_ in range(HT):
                    act.wait_ge(hid_ready, g * HT + t_ + 1)
                    if t_ == 0 and g > DOWN_LAG:
                        act.wait_ge(y_ready, g - DOWN_LAG)
                    nc.scalar.activation(G[g % (DOWN_LAG + 1)][:, t_, :], hid_banks[t_], ACT.Gelu,
                                         bias=BIAS1[:, t_:t_ + 1]).then_inc(gelu_done, 1)
        @block.vector
        def _(dve):
            links = [0]

            def link(op):
                links[0] += 1
                op.then_inc(dve_self, 1)
                dve.wait_ge(dve_self, links[0])

            def lo(dst, src, hi_part):
                return nc.vector.tensor_tensor(dst, src, hi_part.bitcast(F32), ALU.subtract)

            nc.vector.memset(QL[K:P, :, 0, :].bitcast(F32), 0.0)
            nc.vector.memset(QL[0:K, :, 1, :].bitcast(F32), 0.0)
            nc.vector.memset(MP[:], LOWEST).then_inc(rows_set, 1)

            def lay(n):
                what, g = LAY[n]
                bank = lay_banks[n % 4]
                if what == "x":
                    dve.wait_ge(xt_hi, n + 1)
                    op = lo(XTL[:, g * CH:(g + 1) * CH], bank, XTH[:, g * CH:(g + 1) * CH])
                else:
                    dve.wait_ge(laid_made, n + 1)
                    if what == "wo":
                        op = nc.vector.tensor_scalar(WOT[:, g * TPC:(g + 1) * TPC, :],
                                                     bank.rearrange("p (t d) -> p t d", t=TPC), -1.0, None, ALU.mult)
                    else:
                        op = nc.vector.tensor_copy(w2t, bank)
                op.then_inc(laid_copied, 1)

            def compose_up(n):
                st, part = n // 3, n % 3
                if n == 0:
                    dve.wait_ge(in_exp, 16)
                    dve.wait_ge(pv_done, NS * (UNITS - 1) + PV_CREDIT)
                if part == 0:
                    dve.wait_ge(up_in[st], 16)
                if n > 0 and part != 1:
                    dve.wait_ge(up_done, n)
                butterfly_op(nc.vector, W1[:, :], up_scratch, up_w_slot[st], st, True, part).then_inc(up_done, 1)

            for n in range(CHUNKS):
                lay(n)
            dve.wait_ge(in_w, 48)

            def stage_low(col, staged):
                dve.wait_ge(weights_hi, staged.value())
                lo(WST[:, 1, :, :], WQKV[:, :, bass.ds(col, P)], WST[:, 0, :, :]).then_inc(weights_lo, 1)

            stage_low(0, At(1))
            for cr, n in ((exp_done, EXP_CREDIT), (pv_done, PV_CREDIT), (o_free, O_CREDIT)):
                dve.sem_inc(cr, n)

            def consume(f, at, unit, nxt, pair=None):
                w = WORK[at.bank()]
                free = work_free[at.bank()]
                if f[0] == "proj" and f[1] < 2:
                    _, n, c = f
                    done = {(0, 0): 1, (1, 0): 2, (0, 1): 3, (1, 1): 4}[(n, c)]
                    dve.wait_ge(qk_hi, ((unit + 1).times(4) + done).value())
                    cols = slice(c * CH, (c + 1) * CH)
                    A, Bh = slice(0, K), slice(K, P)
                    if n == 0:
                        lo(QL[A, nxt, 0, cols], w[A, :], QH[A, nxt, 0, cols])
                        op = lo(QL[Bh, nxt, 1, cols], w[Bh, :], QH[Bh, nxt, 1, cols])
                    else:
                        lo(KHL[Bh, nxt, 0, cols], w[A, :], KHL[A, nxt, 0, cols])
                        op = lo(KHL[A, nxt, 1, cols], w[Bh, :], KHL[Bh, nxt, 1, cols])
                    op.then_inc(free, 1)
                elif f[0] == "max":
                    pieces = f[1]
                    dve.wait_ge(work_ready, (at + 1).value())
                    dve.sem_inc(dve_passed, 1)
                    at_col = 0
                    for h, qt, part in pieces:
                        _, n = keys_of(part, qt)
                        cell = MP[:, h * TILES + qt, part:part + 1]
                        cols = w[:, at_col:at_col + n]
                        at_col += n
                        if (part + 1) * TPC > qt:
                            op = nc.vector.tensor_tensor_reduce(cols, cols, CMASK[:, CH - n:], 1.0, LOWEST,
                                                                ALU.add, ALU.max, cell)
                        else:
                            op = nc.vector.tensor_reduce(cell, cols, AX_X, ALU.max)
                    op.then_inc(free, 1)
                    if f == MAXES[-1]:
                        dve.wait_ge(free, (at.uses() + 1).value())
                        nc.vector.tensor_reduce(NEGM[:, :], MP[:, :, :], AX_X, ALU.max,
                                                negate=True).then_inc(negm_made, 1)
                elif f[0] == "mt":
                    dve.wait_ge(work_ready, (at + 1).value())
                    if not (at.b is None):
                        dve.wait_ge(m_landed, (unit + 1).times(32).value())
                    nc.vector.tensor_copy(NROW[:, :], w[0:2 * TILES, 0:P]).then_inc(nrow_made, 1)
                    dve.wait_ge(nrow_made, (unit + 2).value())
                    dve.sem_inc(free, 1)
                elif f[0] == "norm":
                    _, qc, back = f
                    norms = (unit + -back).times(CHUNKS) + qc
                    dve.wait_ge(recip_made, (norms + 1).value())
                    nc.vector.tensor_tensor(R[:, :], w[:, :], R0[:, :], ALU.mult).then_inc(free, 1)
                    dve.wait_ge(free, (at.uses() + 1).value())
                    nc.vector.scalar_tensor_tensor(R[:, :], R[:, :], 2.0, R0[:, :], ALU.subtract,
                                                   ALU.mult).then_inc(inverse_made, 1)
                    dve.wait_ge(inverse_made, (norms + 1).value())
                    dst = OT[:, bass.ds(pair, 1), qc * CH:(qc + 1) * CH].rearrange("p a c -> p (a c)")
                    nc.vector.tensor_tensor(dst, O[qc][:, :], R[:, :], ALU.mult).then_inc(o_free, 1)

            def window(b, j, par, kind):
                unit, base = unit_at(b, j, par), work_base(b, j, par, kind)
                mine = par if j is None else j * 2 + par
                queue = fillers(kind)
                for i in reversed(range(len(queue) - 1)):
                    if queue[i][1][0] == "norm" and queue[i + 1][1][0] != "norm":
                        queue[i], queue[i + 1] = queue[i + 1], queue[i]
                for s, f, n, ahead in queue:
                    back = f[2] if f[0] == "norm" else 0
                    consume(f, base + n, unit + (ahead - 1), (par + ahead) % 2, pair=mine - back)
                    if kind == LAST:
                        for step in range(0, 12) if back else range(12, 3 * STAGES):
                            compose_up(step)
                    if f == MAXES[0] and kind in (FIRST, MIDDLE):
                        stage_low(pair_col(j, par, 2), unit + 3)

            dve.wait_ge(consts_set, 1)
            for n, (f, ahead) in enumerate(PREFETCH):
                consume(f, At(n), At(ahead - 2), ahead - 1)
                for job in lays_after(n):
                    lay(job)
                if f == LAST_PROJ:
                    stage_low(P, At(2))
            dve.wait_ge(in_bc, 32)
            nc.vector.tensor_tensor(BC[:, :], BC[:, :], down_row, ALU.add).then_inc(bc_made, 1)
            dve.wait_ge(laid_made, len(LAY) + 1)
            nc.vector.tensor_copy(BIAS1[:, :], lay_banks[len(LAY) % 4][:, 0:HT]).then_inc(laid_copied, 1)

            def normalise(g, done):
                for t in range(g * TPC, (g + 1) * TPC):
                    nc.vector.tensor_scalar(X[:, t, :], X[:, t, :], MV[:, t, 0:1], RSTD[:, t:t + 1],
                                            ALU.subtract, ALU.mult).then_inc(done, 1)

            def copy_x1t(g):
                dve.wait_ge(x1t_made, g + 1)
                nc.vector.tensor_copy(x1T[g % 2], O[g % 2][:, :]).then_inc(x1t_copied, 1)
                xs = X[:, g * TPC:(g + 1) * TPC, :]
                bc = BC[:, :].rearrange("p (a d) -> p a d", a=1).broadcast_to([P, TPC, D])
                link(nc.vector.tensor_tensor(xs, xs, bc, ALU.add))

            def flush(b):
                at = flush_base(b)
                unit = At(PAIRS - 1, PAIRS, 0, b)
                first = 0
                for n, tiles in enumerate(OUT_TILES):
                    if n == 1:
                        consume(("norm", 1, 0), at, unit, 0, pair=PAIRS - 1)
                        at = at + 1
                    if n == 2 and isinstance(b, int) and b == B - 1:
                        dve.wait_ge(rstd_made, 1)
                        for g in range(AHEAD):
                            normalise(g, x1_made)
                    dve.wait_ge(work_ready, (at + 1).value())
                    xs = X[:, bass.ds(b * TILES + first, tiles), :]
                    w = WORK[at.bank()][:, 0:tiles * P].rearrange("p (t d) -> p t d", t=tiles)
                    nc.vector.tensor_tensor(xs, w, xs, ALU.add).then_inc(work_free[at.bank()], 1)
                    dve.wait_ge(work_free[at.bank()], (at.uses() + 1).value())
                    dve.sem_inc(dve_passed, 1)
                    for i in range(tiles):
                        nc.vector.bn_stats(BS[:, i, :], X[:, bass.ds(b * TILES + (first + i), 1), :]
                                           .rearrange("p a d -> p (a d)")).then_inc(h1_added, 1)
                    dve.wait_ge(h1_added, b * TILES + (first + tiles))
                    dve.sem_inc(dve_passed, 1)
                    for i in range(tiles):
                        nc.vector.bn_aggr(MVT[:, i, :], BS[:, i, :]).then_inc(aggregated, 1)
                    dve.wait_ge(aggregated, b * TILES + (first + tiles))
                    nc.vector.tensor_copy(MV[:, bass.ds(b * TILES + first, tiles), :], MVT[:, 0:tiles, :])\
                        .then_inc(stats_made, tiles)
                    first += tiles
                    at = at + 1

            sweep(dve, window, flush)

            def residual(g):
                dve.wait_ge(y_ready, g + 1)
                xs = X[:, g * TPC:(g + 1) * TPC, :]
                nc.vector.tensor_tensor(xs, WORK[g % 2][:, :].rearrange("p (t d) -> p t d", t=TPC), xs,
                                        ALU.add).then_inc(h2_made, 1)
                dve.wait_ge(h2_made, g + 1)
                for i in range(TPC):
                    nc.vector.bn_stats(BS[:, i, :], X[:, g * TPC + i, :]).then_inc(h1_added, 1)
                dve.wait_ge(h1_added, (B * CHUNKS + g + 1) * TPC)
                for i in range(TPC):
                    nc.vector.bn_aggr(MV[:, g * TPC + i, :], BS[:, i, :]).then_inc(stats_made, 1)

            def result(g):
                dve.wait_ge(rstd_made, 2 + g + 1)
                normalise(g, out_made)

            dve.wait_ge(bc_made, 1)

            def compose_down(stages):
                for n in stages:
                    dve.wait_ge(down_in[n], 16)
                    for part in range(3):
                        if part != 1:
                            dve.wait_ge(down_done, 3 * n + part)
                        butterfly_op(nc.vector, w2t, down_scratch, down_w_slot[n], STAGES - 1 - n, False, part)\
                            .then_inc(down_done, 1)

            for g in range(2):
                copy_x1t(g)
            compose_down(range(POOL_STAGES, POOL_STAGES + 2))
            for g in range(B * CHUNKS):
                if g + 2 < B * CHUNKS:
                    copy_x1t(g + 2)
                if g + AHEAD < B * CHUNKS:
                    dve.wait_ge(rstd_made, 2)
                    normalise(g + AHEAD, x1_made)
                if g == 0:
                    compose_down(range(POOL_STAGES + 2, STAGES))
                if g == DOWN_LAG:
                    dve.wait_ge(w2_made, 1)
                    nc.vector.tensor_copy(w2t, WORK[1][:, :]).then_inc(w2_copied, 1)
                if g >= DOWN_LAG:
                    residual(g - DOWN_LAG)
                if g > DOWN_LAG:
                    result(g - DOWN_LAG - 1)
            for g in range(B * CHUNKS - DOWN_LAG, B * CHUNKS):
                residual(g)
                result(g - 1)
            result(B * CHUNKS - 1)


_INS = ["L0_attn_x_BSE", "L0_attn_w_q", "L0_attn_w_k", "L0_attn_w_v", "L0_attn_w_o", "L0_ffn_W_exp", "L0_ffn_b_exp",
        "L0_ffn_up_weights", "L0_ffn_up_bias", "L0_ffn_down_weights", "L0_ffn_W_con", "L0_ffn_b_con",
        "L0_ffn_down_bias"]
_OUTS = [((B, S, D), "float32")]


def kernel(**inputs):
    import numpy as _np
    import concourse.bacc as _bacc
    from concourse import mybir as _mybir
    from concourse.bass_utils import run_bass_kernel_spmd as _run

    nc = _bacc.Bacc("TRN2", target_bir_lowering=False, num_devices=1)
    arrays, args = {}, []
    for name in _INS:
        a = _np.ascontiguousarray(inputs[name])
        arrays[f"in_{name}_dram"] = a
        args.append(nc.dram_tensor(f"in_{name}_dram", a.shape, _mybir.dt.from_np(a.dtype), kind="ExternalInput").ap())
    for i, (shape, dtype) in enumerate(_OUTS):
        dt = _mybir.dt.from_np(_np.dtype(dtype))
        args.append(nc.dram_tensor(f"out_{i}_dram", shape, dt, kind="ExternalOutput").ap())
    post_norm_layer(nc, *args)
    r = _run(nc, [arrays], core_ids=[0])
    got = tuple(r.results[0][f"out_{i}_dram"] for i in range(len(_OUTS)))
    return got[0]
```
